# Optimizing a Trainium2 kernel written in Bass

```python
import numpy as np
import jax
import jax.numpy as jnp

def _softmax(x, axis=-1):
    return jax.nn.softmax(x, axis=axis)

def _gelu(x):
    return jax.nn.gelu(x, approximate=True)

def _silu(x):
    return jax.nn.silu(x)

def _sigmoid(x):
    return jax.nn.sigmoid(x)

def _layernorm(x, axis=-1, eps=1e-05):
    m = jnp.mean(x, axis=axis, keepdims=True)
    v = jnp.var(x, axis=axis, keepdims=True)
    return (x - m) / jnp.sqrt(v + eps)

def _scatter_add(tgt, idx, src, axis=0):
    return tgt.at[idx].add(src)

def _segment_sum(src, seg, n):
    return jax.ops.segment_sum(src, seg, n)
kernel_name = 'mk_seq_postln_d1_jaxref_r8_452bc5'

def setup_inputs(seed: int=0):
    np.random.seed(seed)
    _w = jnp.asarray

    def _L0_attn_setup():
        import jax, jax.numpy as jnp
        import numpy as np
        import math
        EMBED_DIM = 128
        NDIM = 2
        SCALE = math.sqrt(1.0 / NDIM)

        def _ema_kernel(delta, alpha, beta, gamma, length):
            p = jax.nn.sigmoid(delta)
            a = jax.nn.sigmoid(alpha)
            q = 1.0 - p * a
            t = jnp.arange(length, dtype=q.dtype)
            vander = t[None, None, :] * jnp.log(q)
            kernel = p * beta * jnp.exp(vander)
            return jnp.einsum('dnl,dn->dl', kernel, gamma * SCALE)
        key = jax.random.key(seed)
        ks = jax.random.split(key, 6)
        B, S, D, N = (4, 1024, EMBED_DIM, NDIM)
        x = jax.random.normal(ks[0], (B, S, D), dtype=jnp.float32)
        delta = 0.2 * jax.random.normal(ks[1], (D, N, 1), dtype=jnp.float32)
        alpha = 0.2 * jax.random.normal(ks[2], (D, N, 1), dtype=jnp.float32)
        val = jnp.where(jnp.arange(N) % 2 == 1, -1.0, 1.0).reshape(N, 1).astype(jnp.float32)
        beta = 0.02 * jax.random.normal(ks[3], (D, N, 1), dtype=jnp.float32) + val
        gamma = jax.random.normal(ks[4], (D, N), dtype=jnp.float32)
        omega = jax.random.normal(ks[5], (D,), dtype=jnp.float32)
        return {'x': x, 'delta': delta, 'alpha': alpha, 'beta': beta, 'gamma': gamma, 'omega': omega}
    _L0_attn_in = _L0_attn_setup()

    def _L0_ffn_setup():
        import jax, jax.numpy as jnp
        import numpy as np
        B, S, H = (8, 128, 128)
        FF = 512
        E = 8
        TOP_K = 2
        LN_EPS = 1e-12

        def _layernorm(x, w, b):
            mu = jnp.mean(x, axis=-1, keepdims=True)
            var = jnp.mean(jnp.square(x - mu), axis=-1, keepdims=True)
            return (x - mu) * jax.lax.rsqrt(var + LN_EPS) * w + b
        key = jax.random.key(seed)
        ks = jax.random.split(key, 8)
        sc_h = 1.0 / np.sqrt(H)
        sc_ff = 1.0 / np.sqrt(FF)
        return {'hidden_states': jax.random.normal(ks[0], (B, S, H), jnp.float32), 'router_w': jax.random.normal(ks[1], (E, H), jnp.float32) * sc_h, 'router_b': jnp.zeros((E,), jnp.float32), 'w1': jax.random.normal(ks[2], (E, FF, H), jnp.float32) * sc_h, 'b1': jax.random.normal(ks[3], (E, FF), jnp.float32) * 0.01, 'w2': jax.random.normal(ks[4], (E, H, FF), jnp.float32) * sc_ff, 'b2': jax.random.normal(ks[5], (E, H), jnp.float32) * 0.01, 'ln_w': jnp.ones((H,), jnp.float32), 'ln_b': jnp.zeros((H,), jnp.float32)}
    _L0_ffn_in = _L0_ffn_setup()
    _d = {'L0_attn_x': _L0_attn_in['x'], 'L0_attn_delta': _L0_attn_in['delta'], 'L0_attn_alpha': _L0_attn_in['alpha'], 'L0_attn_beta': _L0_attn_in['beta'], 'L0_attn_gamma': _L0_attn_in['gamma'], 'L0_attn_omega': _L0_attn_in['omega'], 'L0_ffn_router_w': _L0_ffn_in['router_w'], 'L0_ffn_router_b': _L0_ffn_in['router_b'], 'L0_ffn_w1': _L0_ffn_in['w1'], 'L0_ffn_b1': _L0_ffn_in['b1'], 'L0_ffn_w2': _L0_ffn_in['w2'], 'L0_ffn_b2': _L0_ffn_in['b2'], 'L0_ffn_ln_w': _L0_ffn_in['ln_w'], 'L0_ffn_ln_b': _L0_ffn_in['ln_b']}
    _x0 = _d['L0_attn_x']
    _d['L0_attn_x'] = jax.random.normal(jax.random.fold_in(jax.random.key(seed), 1), (4, 1024, 128), dtype=_x0.dtype)
    del _x0
    return _d

def reference(L0_attn_x, L0_attn_delta, L0_attn_alpha, L0_attn_beta, L0_attn_gamma, L0_attn_omega, L0_ffn_router_w, L0_ffn_router_b, L0_ffn_w1, L0_ffn_b1, L0_ffn_w2, L0_ffn_b2, L0_ffn_ln_w, L0_ffn_ln_b):

    def _L0_attn_ref(x, delta, alpha, beta, gamma, omega):
        import jax, jax.numpy as jnp
        import numpy as np
        import math
        EMBED_DIM = 128
        NDIM = 2
        SCALE = math.sqrt(1.0 / NDIM)

        def _ema_kernel(delta, alpha, beta, gamma, length):
            p = jax.nn.sigmoid(delta)
            a = jax.nn.sigmoid(alpha)
            q = 1.0 - p * a
            t = jnp.arange(length, dtype=q.dtype)
            vander = t[None, None, :] * jnp.log(q)
            kernel = p * beta * jnp.exp(vander)
            return jnp.einsum('dnl,dn->dl', kernel, gamma * SCALE)
        B, S, D = x.shape
        residual = x * omega
        xt = jnp.transpose(x, (0, 2, 1))
        k = _ema_kernel(delta, alpha, beta, gamma, S)
        n = 2 * S
        k_f = jnp.fft.rfft(k.astype(jnp.float32), n=n)
        x_f = jnp.fft.rfft(xt.astype(jnp.float32), n=n)
        out = jnp.fft.irfft(x_f * k_f, n=n)[..., :S]
        out = out.astype(x.dtype)
        return jax.nn.silu(jnp.transpose(out, (0, 2, 1)) + residual)

    def _L0_ffn_ref(hidden_states, router_w, router_b, w1, b1, w2, b2, ln_w, ln_b):
        import jax, jax.numpy as jnp
        import numpy as np
        B, S, H = (8, 128, 128)
        FF = 512
        E = 8
        TOP_K = 2
        LN_EPS = 1e-12

        def _layernorm(x, w, b):
            mu = jnp.mean(x, axis=-1, keepdims=True)
            var = jnp.mean(jnp.square(x - mu), axis=-1, keepdims=True)
            return (x - mu) * jax.lax.rsqrt(var + LN_EPS) * w + b
        b, s, h = hidden_states.shape
        flat = hidden_states.reshape(-1, h)
        logits = flat @ router_w.T + router_b
        topk_vals, topk_idx = jax.lax.top_k(logits, TOP_K)
        topk_w = jax.nn.softmax(topk_vals, axis=-1)
        out = jnp.zeros_like(flat)
        n_exp = w1.shape[0]
        for e in range(n_exp):
            cw = jnp.sum(jnp.where(topk_idx == e, topk_w, 0.0), axis=-1)
            y = jax.nn.gelu(flat @ w1[e].T + b1[e], approximate=False)
            y = y @ w2[e].T + b2[e]
            out = out + y * cw[:, None]
        out = out.reshape(b, s, h) + hidden_states
        return _layernorm(out, ln_w, ln_b)
    x = L0_attn_x
    x = _layernorm(x + _L0_attn_ref(x, L0_attn_delta, L0_attn_alpha, L0_attn_beta, L0_attn_gamma, L0_attn_omega), axis=-1)
    x = _layernorm(x + _L0_ffn_ref(x, L0_ffn_router_w, L0_ffn_router_b, L0_ffn_w1, L0_ffn_b1, L0_ffn_w2, L0_ffn_b2, L0_ffn_ln_w, L0_ffn_ln_b), axis=-1)
    return x

_drawn_inputs = setup_inputs


def setup_inputs(seed=0):
    import zlib

    import numpy as np

    out = dict(_drawn_inputs(seed))
    spreads = {'L0_ffn_router_b': (0.0, 0.1), 'L0_ffn_ln_w': (1.0, 0.2), 'L0_ffn_ln_b': (0.0, 0.1)}
    factors = {'L0_attn_beta': 3.606, 'L0_ffn_b1': 23.146, 'L0_ffn_b2': 8.0}
    for name, (base, spread) in spreads.items():
        noise = np.random.default_rng([zlib.crc32(name.encode()), seed]).standard_normal(out[name].shape)
        drawn = base * np.exp(spread * noise) if base else spread * noise
        out[name] = jnp.asarray(drawn.astype(out[name].dtype))
    for name, factor in factors.items():
        out[name] = (out[name] * factor).astype(out[name].dtype)
    return out
```

```python
import math
from contextlib import ExitStack

import concourse.bass as bass
from concourse import mybir

f32 = mybir.dt.float32
f32r = mybir.dt.float32r
bf16 = mybir.dt.bfloat16
i32 = mybir.dt.int32
ALU = mybir.AluOpType
ACT = mybir.ActivationFunctionType
AX = mybir.AxisListType

P = 128
BATCH, SEQ, D = 4, 1024, 128
T = BATCH * SEQ
E, FF, TOP = 8, 512, 2
FC = FF // P
CH = 2 * P
NCH = T // CH
NT = T // P
CB = SEQ // CH
SCALE = math.sqrt(0.5)
LN_EPS, FFN_EPS = 1e-5, 1e-12
BIG = 3.0e38

GROUPS = [4, 8, 14, 6]
G = len(GROUPS)
T0 = [sum(GROUPS[:g]) for g in range(G + 1)]
SLOTS = [TOP * m + E - 1 for m in GROUPS]
N0 = [sum(SLOTS[:g]) for g in range(G + 1)]
NS = N0[G]
PAIRS = NS // 2
assert T0[G] == NT and NS % 2 == 0 and all(m % 2 == 0 for m in GROUPS)

SCHEDULE = [
    ("A", 0, 2), ("R", 0), ("A", 2, 4), ("R", 1),
    ("AC", 0, 7, 6), ("R", 2), ("AC", 7, 3, 13), ("R", 3),
    ("C", 10, 2), ("DC", 12, 2, 0), ("C", 14, 8), ("DC", 22, 4, 2), ("C", 26, 13), ("DC", 39, 7, 6),
    ("D", 13, 3),
]
POOL = [("a", 0), ("a", 1), ("S", 0, 0, 8)] + [("a", a) for a in range(2, 6)]
for _k in range(5):
    POOL += [("S", 1, 3 * _k, 3), ("a", 6 + _k)]
POOL += [("S", 1, 15, 1), ("a", 11), ("a", 12)]
for _k in range(3):
    POOL += [("S", 2, 3 * _k, 3), ("a", 13 + _k)]
POOL += [("S", 2, 9, 19), ("g", 0), ("g", 1), ("1", 0), ("2", 0), ("1", 1), ("S", 3, 0, 12)]
POOL += [("g", 2), ("g", 3), ("2", 1), ("1", 2), ("g", 4), ("2", 2), ("1", 3), ("g", 5), ("2", 3), ("1", 4),
         ("2", 4), ("1", 5)]
POOL += [("g", 6), ("g", 7), ("2", 5), ("1", 6)]
for _d in range(7, 13):
    POOL += ([("g", _d + 1)] if _d < 12 else []) + [("2", _d - 1), ("1", _d)]
POOL += [("g", 13), ("2", 12), ("1", 13), ("g", 14), ("2", 13), ("1", 14), ("g", 15), ("2", 14), ("1", 15), ("2", 15)]

PREP_DVE = 12


def at_least(eng, sem, value):
    if not (isinstance(value, int) and value <= 0):
        eng.wait_ge(sem, value)


def repeat(eng, lo, hi, body):
    if hi - lo <= 1:
        for i in range(lo, hi):
            body(i)
    else:
        with eng.Fori(lo, hi) as i:
            body(i)


def segment(eng, n, body, last_apart=False, first=1):
    for i in range(first):
        body(i)
    hi = n - 1 if last_apart and n > 1 else n
    repeat(eng, first, hi, body)
    if hi < n:
        body(n - 1)


def ema_moe_kernel(nc, xT, prm, rows, rwT, w1T, w2T, b1, b2, out):
    xs_dram = nc.dram_tensor("slots_in", [NS * P, D], f32).ap()
    y_dram = nc.dram_tensor("slots_out", [NS * P, D], f32).ap()
    bias_dram = nc.dram_tensor("bias_parts", [3, E * FF + E * D], bf16).ap()

    ctx = ExitStack()
    with ctx:
        def sb(name, shape, dt=f32):
            return ctx.enter_context(nc.sbuf_tensor(name, shape, dt))

        def sem(name):
            return ctx.enter_context(nc.semaphore(name))

        x_sb = sb("x_sb", [P, T])
        x2 = sb("x2", [P, NT, D])
        w1h, w1l = sb("w1h", [P, E * FF], f32r), sb("w1l", [P, E * FF], f32r)
        w2 = sb("w2", [P, E * FF])
        yg = sb("yg", [P, NCH, 2 * TOP, D])
        stage = yg[:, :, :, :].rearrange("p a b c -> p (a b c)")
        bias = sb("bias", [P, 2, E, FF], bf16)
        b1_rows, b2_rows = (bias[:, k].rearrange("p e f -> p (e f)") for k in range(2))
        bcol = sb("bcol", [P, 40])
        bpart = sb("bpart", [P, 3, 40], bf16)
        prm_sb = sb("prm_sb", [P, 9])
        row_sb = sb("row_sb", [P, E + 2 * D])
        rb, lnw, lnb = row_sb[:, 0:E], row_sb[:, E:E + D], row_sb[:, E + D:E + 2 * D]
        rw_sb, rwc = sb("rw_sb", [P, E]), sb("rwc", [P, E])
        zeros = sb("zeros", [P, 8 * D])
        ident, centre = sb("ident", [P, P]), sb("centre", [P, P])
        ones, before = sb("ones", [P, P], bf16), sb("before", [P, P], bf16)
        power = sb("power", [P, 2])
        pa, q, cf, om = sb("pa", [P, 4]), sb("q", [P, 2]), sb("cf", [P, 2]), sb("om", [P, 1])
        keep = sb("keep", [P, NCH + 1])
        carry = sb("carry", [P, 2])
        h = sb("h", [P, 2, CH])
        t1, t2, v, th, p, s = (sb(n, [P, CH]) for n in ("t1", "t2", "v", "th", "p", "s"))
        st_a, mv_a, ve_a, rs_a = sb("st_a", [P, 2, 6]), sb("mv_a", [P, 2, 2]), sb("ve_a", [P, 2]), sb("rs_a", [P, 2])
        M = max(GROUPS)
        logit = sb("logit", [P, NT, E])
        oh = [sb("oh1", [P, M, E]), sb("oh2", [P, M, E])]
        ra, rk = sb("ra", [P, M, E]), sb("rk", [P, M, E])
        rm = [sb("rm1", [P, M]), sb("rm2", [P, M])]
        rkm, rd, rth = sb("rkm", [P, M]), sb("rd", [P, M]), sb("rth", [P, M])
        both = sb("both", [P, M, E], bf16)
        tot, inc = sb("tot", [P, E, M]), sb("inc", [P, E, M])
        nti, ends, base = sb("nti", [P, E]), sb("ends", [P, E]), sb("base", [P, E])
        fill = sb("fill", [P, E, M])
        spos = sb("spos", [P, M, E])
        slotf = sb("slotf", [P, TOP, M])
        slots = sb("slots", [P, TOP, NT], i32)
        wts = sb("wts", [P, TOP, NT])
        rev = sb("rev", [P, E])
        k128 = sb("k128", [P, M])
        restart = {m: sb(f"restart{m}", [P, E * m]) for m in sorted(set(GROUPS))}
        JM = max(SLOTS)
        jidx, ecmp, esum = sb("jidx", [1, JM]), sb("ecmp", [1, JM, E]), sb("esum", [1, JM])
        eid = sb("eid", [1, PAIRS + 1, 4], i32)
        xs = sb("xs", [P, 2, D])
        xh, xl = sb("xh", [P, 2 * P], f32r), sb("xl", [P, 2 * P], f32r)
        g = [sb(f"g{k}", [P, FF]) for k in range(2)]
        gt = [sb(f"gt{k}", [P, FF]) for k in range(2)]
        y_sb = sb("y_sb", [P, 2, D])
        z, zn, u = sb("z", [P, 2, D]), sb("zn", [P, 2, D]), sb("u", [P, 2, D])
        o_sb = sb("o_sb", [P, 2, D])
        st_d = [sb(f"st_d{k}", [P, 2, 6]) for k in range(2)]
        mv_d = [sb(f"mv_d{k}", [P, 2, 2]) for k in range(2)]
        ve_d = [sb(f"ve_d{k}", [P, 2]) for k in range(2)]
        rs_d = [sb(f"rs_d{k}", [P, 2]) for k in range(2)]

        def pb(name):
            return ctx.enter_context(nc.psum_tensor(name, [P, 512], f32))

        bank_a, bank_x = pb("bank_a"), pb("bank_x")
        bank_z = [pb(f"bank_z{k}") for k in range(2)]
        bank_g = [pb(f"bank_g{k}") for k in range(2)]
        bank_y = [pb(f"bank_y{k}") for k in range(2)]
        pace = sb("pace", [P, 1])
        stok = bank_a[:, 0:CH]
        raw = bank_a[:, CH:CH + 2 * E]

        prm_in, row_in, rw_in, b_in = sem("prm_in"), sem("row_in"), sem("rw_in"), sem("b_in")
        x_in = [sem(f"x_in{k}") for k in range(4)]
        w_in = [sem(f"w_in{k}") for k in range(4)]
        bias_out, bias_back, cleared = sem("bias_out"), sem("bias_back"), sem("cleared")
        const = sem("const")
        pa_tanh = sem("pa_tanh")
        prep = sem("prep")
        rwc_ps = sem("rwc_ps")
        whigh, wlow = sem("whigh"), sem("wlow")
        h1_ready, h2_ready, carry_ready = sem("h1_ready"), sem("h2_ready"), sem("carry_ready")
        t1_ready, t2_ready, v_ready, th_ready = sem("t1_ready"), sem("t2_ready"), sem("v_ready"), sem("th_ready")
        p_ready, s_ready, stok_ready = sem("p_ready"), sem("s_ready"), sem("stok_ready")
        st_ready, mv_ready, ve_ready, rs_ready = sem("st_ready"), sem("mv_ready"), sem("ve_ready"), sem("rs_ready")
        x2_ready = sem("x2_ready")
        route = sem("route")
        both_ready, counted, rd_ready, rth_ready = sem("both_ready"), sem("counted"), sem("rd_ready"), sem("rth_ready")
        slots_ready = sem("slots_ready")
        scattered = [sem(f"scattered{k}") for k in range(G)]
        xs_in, xsT_ready, xh_ready, xl_ready = sem("xs_in"), sem("xsT_ready"), sem("xh_ready"), sem("xl_ready")
        z_ready, g_ready, gT_ready = sem("z_ready"), sem("g_ready"), sem("gT_ready")
        gt_ready, y_ready, y_moved = sem("gt_ready"), sem("y_ready"), sem("y_moved")
        y_out = sem("y_out")
        gathering = [sem(f"gathering{k}") for k in range(2)]
        gathered = sem("gathered")
        za_ready, z_done, dst_ready = sem("za_ready"), sem("z_done"), sem("dst_ready")
        dmv_ready, var1_ready, rs1_ready = sem("dmv_ready"), sem("var1_ready"), sem("rs1_ready")
        zn_ready, zw_ready, ub_ready, u_ready = sem("zn_ready"), sem("zw_ready"), sem("ub_ready"), sem("u_ready")
        dst2_ready, dmv2_ready = sem("dst2_ready"), sem("dmv2_ready")
        var2_ready, rs2_ready, o_ready, o_out = sem("var2_ready"), sem("rs2_ready"), sem("o_ready"), sem("o_out")

        block = ctx.enter_context(nc.Block())

        @block.sync
        def _(sp):
            sp.dma_start(prm_sb[:], prm).then_inc(prm_in, 16)
            XP = T // 4
            sp.dma_start(x_sb[:, 0:XP], xT[:, 0:XP]).then_inc(x_in[0], 16)
            sp.dma_start(rw_sb[:], rwT).then_inc(rw_in, 16)
            sp.dma_start(row_sb[:], rows.to_broadcast([P, E + 2 * D])).then_inc(row_in, 16)
            sp.dma_start(bcol[:, 0:32], b1).then_inc(b_in, 16)
            sp.dma_start(bcol[:, 32:40], b2).then_inc(b_in, 16)
            sp.wait_ge(const, 1)
            for n in range(0, NS, 8):
                k = min(8, NS - n)
                sp.dma_start(xs_dram[n * P:(n + k) * P, :].rearrange("(p r) d -> p (r d)", p=P),
                             zeros[:, 0:k * D]).then_inc(cleared, 16)
                if n == 8:
                    sp.dma_start(x_sb[:, XP:2 * XP], xT[:, XP:2 * XP]).then_inc(x_in[1], 16)
                    for k in range(4):
                        cols = slice(k * 2048, (k + 1) * 2048)
                        if k < 2:
                            sp.dma_start(stage[:, cols], w1T[:, cols]).then_inc(w_in[k], 16)
                        else:
                            cols = slice((k - 2) * 2048, (k - 1) * 2048)
                            sp.dma_start(w2[:, cols], w2T[:, cols]).then_inc(w_in[k], 16)
                    for k in range(2, 4):
                        sp.dma_start(x_sb[:, k * XP:(k + 1) * XP], xT[:, k * XP:(k + 1) * XP]).then_inc(x_in[k], 16)
                    sp.wait_ge(prep, PREP_DVE)
                    for r in range(3):
                        sp.dma_start(bias_dram[r, 0:E * FF].rearrange("(p c) -> p c", p=P),
                                     bpart[:, r, 0:32]).then_inc(bias_out, 16)
                        sp.dma_start(bias_dram[r, E * FF:].rearrange("(p c) -> p c", p=P),
                                     bpart[:, r, 32:40]).then_inc(bias_out, 16)
                    sp.wait_ge(bias_out, 6 * 16)
                    sp.wait_ge(const, 3)
                    sp.dma_start(b1_rows[0:3, :], bias_dram[:, 0:E * FF]).then_inc(bias_back, 16)
                    sp.dma_start(bias[0:3, 1, :, 0:D], bias_dram[:, E * FF:].rearrange("r (e d) -> r e d", e=E))\
                        .then_inc(bias_back, 16)

            def load(b):
                at_least(sp, xsT_ready, b)
                sp.dma_start(xs[:], xs_dram[bass.ds(b * 2 * P, 2 * P), :].rearrange("(k p) d -> p k d", p=P))\
                    .then_inc(xs_in, 16)

            def store_y(b):
                sp.wait_ge(y_moved, 2 * b + 2)
                sp.dma_start(y_dram[bass.ds(b * 2 * P, 2 * P), :].rearrange("(k p) d -> p k d", p=P), y_sb[:])\
                    .then_inc(y_out, 16)

            def store_o(d):
                sp.wait_ge(o_ready, d + 1)
                sp.dma_start(out[bass.ds(d * CH, CH), :].rearrange("(k p) d -> p k d", p=P), o_sb[:])\
                    .then_inc(o_out, 16)

            def group_wait(b):
                for k in range(G):
                    if N0[k] // 2 == b:
                        sp.wait_ge(scattered[k], 16 * TOP * GROUPS[k])

            first_of = [N0[k] // 2 for k in range(G)]

            def pairs(b0, n, d0=None):
                at = b0
                while at < b0 + n:
                    if at + 2 in first_of and at + 2 < PAIRS:
                        group_wait(at + 2)
                    end = at + 1
                    while end < b0 + n and end + 2 not in first_of and (end + 2 < PAIRS) == (at + 2 < PAIRS) \
                            and at >= 1 and (d0 != 0 or at >= b0 + 2):
                        end += 1

                    def body(b, at=at):
                        if at + 2 < PAIRS:
                            load(b + 2)
                        if at >= 1:
                            store_y(b - 1)
                        if d0 is not None and not (d0 == 0 and at < b0 + 2):
                            store_o(b - b0 + d0 - 2)
                    repeat(sp, at, end, body)
                    at = end

            group_wait(0)
            load(0)
            load(1)
            for seg in SCHEDULE:
                if seg[0] in ("C", "AC"):
                    pairs(seg[1], seg[2])
                elif seg[0] == "DC":
                    _, b0, n, d0 = seg
                    pairs(b0, n, d0)
                    if b0 + n == PAIRS:
                        store_y(PAIRS - 1)
                elif seg[0] == "D":
                    repeat(sp, seg[1] - 2, NCH, store_o)
            sp.wait_ge(o_out, 16 * NCH)

        @block.gpsimd
        def _(pool):
            pool.memset(zeros[:], 0.0).then_inc(const, 1)
            pool.memset(b1_rows, 0.0).then_inc(const, 1)
            pool.memset(bias[:, 1, :, 0:D], 0.0).then_inc(const, 1)
            pool.memset(ident[:], 0.0).then_inc(const, 1)
            pool.memset(ones[:], 1.0).then_inc(const, 1)
            pool.wait_ge(const, 5)
            pool.affine_select(out=ident[:], in_=ident[:], compare_op=ALU.not_equal, fill=1.0, base=0,
                               pattern=[[-1, P]], channel_multiplier=1).then_inc(const, 1)
            pool.affine_select(out=before[:], in_=ones[:], compare_op=ALU.is_gt, fill=0.0, base=0,
                               pattern=[[1, P]], channel_multiplier=-1).then_inc(const, 1)
            pool.memset(power[:], -0.5).then_inc(const, 1)
            imprecise = dict(channel_multiplier=0, allow_small_or_imprecise_dtypes=True)
            pool.iota(rev[:], pattern=[[-1, E]], base=E, **imprecise).then_inc(const, 1)
            pool.iota(k128[:], pattern=[[P, M]], base=0, **imprecise).then_inc(const, 1)
            pool.iota(jidx[:], pattern=[[1, JM]], base=0, **imprecise).then_inc(const, 1)

            def scatter(gr, k0, n):
                if k0 == 0:
                    pool.wait_ge(slots_ready, gr + 1)
                    if gr == 0:
                        pool.wait_ge(cleared, 16 * -(-NS // 8))
                for k in range(k0, k0 + n):
                    t, top = T0[gr] + k // TOP, k % TOP
                    pool.indirect_dma_start(
                        out=xs_dram, out_offset=bass.IndirectOffsetOnAxis(ap=slots[:, top, t:t + 1], axis=0),
                        in_=x2[:, t, :], in_offset=None, bounds_check=NS * P - 1, oob_is_err=False,
                    ).then_inc(scattered[gr], 16)

            def gather(d):
                written = next(N0[gr + 1] * P for gr in range(G) if 2 * d < T0[gr + 1])
                for gr in range(G):
                    if 2 * d == T0[gr]:
                        pool.wait_ge(y_out, 16 * ((N0[gr + 1] - 1) // 2 + 1))
                if d >= 2:
                    pool.wait_ge(gathering[d % 2], 64 * (d // 2))
                for k in range(2):
                    for top in range(TOP):
                        pool.indirect_dma_start(
                            out=yg[:, d, 2 * k + top, :], out_offset=None, in_=y_dram[0:written, :],
                            in_offset=bass.IndirectOffsetOnAxis(ap=slots[:, top, 2 * d + k:2 * d + k + 1], axis=0),
                            bounds_check=written - 1, oob_is_err=False,
                        ).then_inc(gathering[d % 2], 16)

            for item in POOL:
                kind, d = item[0], item[1]
                if kind == "a":
                    pool.wait_ge(ve_ready, d + 1)
                    pool.tensor_tensor(rs_a[:], ve_a[:], power[:], ALU.pow).then_inc(rs_ready, 1)
                elif kind == "S":
                    scatter(*item[1:])
                elif kind == "g":
                    gather(d)
                elif kind == "1":
                    pool.wait_ge(gathering[d % 2], 64 * (d // 2 + 1))
                    pool.engine_nop().then_inc(gathered, 1)
                    pool.wait_ge(var1_ready, d + 1)
                    pool.tensor_tensor(rs_d[0][:], ve_d[0][:], power[:], ALU.pow).then_inc(rs1_ready, 1)
                else:
                    pool.wait_ge(var2_ready, d + 1)
                    pool.tensor_tensor(rs_d[1][:], ve_d[1][:], power[:], ALU.pow).then_inc(rs2_ready, 1)

        @block.scalar
        def _(act):
            act.wait_ge(prm_in, 16)
            act.activation(pa[:], prm_sb[:, 0:4], ACT.Tanh, scale=0.5).then_inc(pa_tanh, 1)

            def split_high():
                for k in range(2):
                    cols = slice(k * 2048, (k + 1) * 2048)
                    act.wait_ge(w_in[k], 16)
                    act.activation(w1h[:, cols], stage[:, cols], ACT.Copy).then_inc(whigh, 1)

            def scale_h1(a):
                act.wait_ge(h1_ready, a + 1)
                if isinstance(a, int) and a == 0:
                    act.wait_ge(prep, 6)
                else:
                    act.wait_ge(t2_ready, a)
                act.activation(t1[:], h[:, 0, :], ACT.Copy, scale=cf[:, 0:1]).then_inc(t1_ready, 1)

            def tanh_v(a):
                act.wait_ge(v_ready, a + 1)
                at_least(act, p_ready, a)
                act.activation(th[:], v[:], ACT.Tanh).then_inc(th_ready, 1)

            def high_x(b):
                act.wait_ge(xsT_ready, b + 1)
                act.activation(xh[:], bank_x[:, 0:2 * P], ACT.Copy).then_inc(xh_ready, 1)

            def gelu(n, k):
                act.wait_ge(z_ready, n + 1)
                act.activation(g[k][:], bank_z[k][:], ACT.Gelu).then_inc(g_ready, 1)

            def move_g(n, k):
                act.wait_ge(gT_ready, n + 1)
                act.activation(gt[k][:], bank_g[k][:], ACT.Copy).then_inc(gt_ready, 1)

            def move_y(n, k, first=False):
                act.wait_ge(y_ready, n + 1)
                if k == 0 and not first:
                    act.wait_ge(y_out, 8 * n)
                act.activation(y_sb[:, k, :], bank_y[k][:, 0:D], ACT.Copy).then_inc(y_moved, 1)

            def pair(b, a=None):
                first, last = isinstance(b, int) and b == 0, isinstance(b, int) and b == PAIRS - 1
                if a is not None:
                    scale_h1(a)
                gelu(2 * b, 0)
                if not first:
                    move_g(2 * b - 1, 1)
                if a is not None:
                    tanh_v(a)
                if not last:
                    high_x(b + 1)
                gelu(2 * b + 1, 1)
                move_g(2 * b, 0)
                if not first:
                    move_y(2 * b - 2, 0, first=isinstance(b, int) and b == 1)
                    move_y(2 * b - 1, 1)

            groups_routed = 0
            for seg in SCHEDULE:
                kind = seg[0]
                if kind == "A":
                    repeat(act, seg[1], seg[1] + 1, lambda a: (scale_h1(a), tanh_v(a)))
                    repeat(act, seg[1] + 1, seg[1] + seg[2], lambda a: (scale_h1(a), tanh_v(a)))
                elif kind == "R":
                    gr = seg[1]
                    act.wait_ge(rd_ready, gr + 1)
                    act.activation(rth[:, 0:GROUPS[gr]], rd[:, 0:GROUPS[gr]], ACT.Tanh, scale=0.5)\
                        .then_inc(rth_ready, 1)
                    if gr == 0:
                        split_high()
                    if gr == 1:
                        high_x(0)
                elif kind == "AC":
                    _, b0, n, a0 = seg
                    segment(act, n, lambda i, b0=b0, a0=a0: pair(b0 + i, a0 + i), first=2 if b0 == 0 else 1)
                elif kind == "C":
                    segment(act, seg[2], lambda i, b0=seg[1]: pair(b0 + i), seg[1] + seg[2] == PAIRS)
                elif kind == "DC":
                    _, b0, n, d0 = seg
                    segment(act, n, lambda i, b0=b0: pair(b0 + i), b0 + n == PAIRS)
                    if b0 + n == PAIRS:
                        move_g(NS - 1, 1)
                        move_y(NS - 2, 0)
                        move_y(NS - 1, 1)

        @block.tensor
        def _(pe):
            pe.wait_ge(prep, 7)
            pe.wait_ge(rw_in, 16)
            pe.matmul(bank_a[:, 0:E], centre[:], rw_sb[:], start=True, stop=True).then_inc(rwc_ps, 1)
            pe.wait_ge(prep, 8)

            def turn_s(a):
                pe.wait_ge(s_ready, a + 1)
                at_least(pe, x2_ready, a)
                for k in range(2):
                    pe.transpose(stok[:, k * P:(k + 1) * P], s[:, k * P:(k + 1) * P], ident[:])
                for k in range(2):
                    last = pe.matmul(raw[:, k * E:(k + 1) * E], s[:, k * P:(k + 1) * P], rwc[:], start=True, stop=True)
                last.then_inc(stok_ready, 1)

            def turn_x(b):
                pe.wait_ge(xs_in, 16 * (b + 1))
                at_least(pe, xl_ready, b)
                for k in range(2):
                    last = pe.transpose(bank_x[:, k * P:(k + 1) * P], xs[:, k, :], ident[:])
                last.then_inc(xsT_ready, 1)

            def experts(b):
                _, values = nc.values_load_multi_w_load_instructions(
                    eid[0:1, bass.ds(b, 1), :], engines=[mybir.EngineType.PE], min_val=0, max_val=(E - 1) * FF,
                    skip_runtime_bounds_check_because="counts of experts, kept to E - 1 by a minimum on the chip")
                return values

            def up(b, k, e):
                cols = bass.ds(e, FF)
                if k == 0:
                    pe.wait_ge(xl_ready, b + 1)
                at_least(pe, g_ready, 2 * b + k - 1)
                xhk, xlk = xh[:, k * P:(k + 1) * P], xl[:, k * P:(k + 1) * P]
                zb = bank_z[k][:]
                pe.matmul(zb, xhk, w1h[:, cols], start=True, stop=False)
                pe.matmul(zb, xhk, w1l[:, cols], start=False, stop=False)
                pe.matmul(zb, xlk, w1h[:, cols], start=False, stop=False)
                pe.matmul(zb, ones[:], b1_rows[:, cols], start=False, stop=True).then_inc(z_ready, 1)

            def turn_g(n, k):
                pe.wait_ge(g_ready, n + 1)
                at_least(pe, gt_ready, n - 1)
                for c in range(FC):
                    last = pe.transpose(bank_g[k][:, c * P:(c + 1) * P], g[k][:, c * P:(c + 1) * P], ident[:])
                last.then_inc(gT_ready, 1)

            def down(n, k, e):
                pe.wait_ge(gt_ready, n + 1)
                at_least(pe, y_moved, n - 1)
                yb = bank_y[k][:, 0:D]
                for c in range(FC):
                    pe.matmul(yb, gt[k][:, c * P:(c + 1) * P], w2[:, bass.ds(e + c * P, P)],
                              start=(c == 0), stop=False)
                pe.matmul(yb, ones[:], b2_rows[:, bass.ds(e, D)], start=False, stop=True)\
                    .then_inc(y_ready, 1)

            def pair(b, a=None):
                first, last = isinstance(b, int) and b == 0, isinstance(b, int) and b == PAIRS - 1
                before0, before1, own0, own1 = experts(b)
                up(b, 0, own0)
                if not first:
                    turn_g(2 * b - 1, 1)
                    down(2 * b - 2, 0, before0)
                up(b, 1, own1)
                if not last:
                    turn_x(b + 1)
                turn_g(2 * b, 0)
                if not first:
                    down(2 * b - 1, 1, before1)
                if a is not None:
                    turn_s(a)

            for seg in SCHEDULE:
                kind = seg[0]
                if kind == "A":
                    segment(pe, seg[2], lambda i, a0=seg[1]: turn_s(a0 + i))
                elif kind == "R":
                    gr = seg[1]
                    m = GROUPS[gr]
                    pe.wait_ge(both_ready, gr + 1)
                    pe.wait_ge(x2_ready, T0[gr + 1] // 2)
                    mm = both[:].rearrange("p t e -> p (t e)")[:, 0:m * E]
                    pe.matmul(bank_a[:, 0:m * E], before[:], mm, start=True, stop=True)
                    pe.matmul(bank_a[:, P:P + m * E], ones[:], mm, start=True, stop=True).then_inc(counted, 1)
                    pe.wait_ge(slots_ready, gr + 1)
                    if gr == 1:
                        turn_x(0)
                        pe.wait_ge(wlow, 2)
                        for k in range(2, 4):
                            pe.wait_ge(w_in[k], 16)
                        pe.wait_ge(bias_back, 32)
                elif kind == "AC":
                    _, b0, n, a0 = seg
                    segment(pe, n, lambda i, b0=b0, a0=a0: pair(b0 + i, a0 + i), first=2 if b0 == 0 else 1)
                elif kind == "C":
                    segment(pe, seg[2], lambda i, b0=seg[1]: pair(b0 + i), seg[1] + seg[2] == PAIRS)
                elif kind == "DC":
                    _, b0, n, d0 = seg
                    segment(pe, n, lambda i, b0=b0: pair(b0 + i), b0 + n == PAIRS)
                    if b0 + n == PAIRS:
                        turn_g(NS - 1, 1)
                        before0, before1, _, _ = experts(PAIRS)
                        down(NS - 2, 0, before0)
                        down(NS - 1, 1, before1)

        @block.vector
        def _(dve):
            steps = [0]

            def prepared(ins):
                ins.then_inc(prep, 1)
                steps[0] += 1

            dve.memset(carry[:], 0.0).then_inc(carry_ready, 1)
            dve.memset(keep[:], 1.0).then_inc(route, 1)
            dve.memset(eid[:], 0).then_inc(route, 1)
            for m in restart:
                dve.memset(restart[m][:], 1.0).then_inc(route, 1)
            ROUTE0 = 2 + len(restart)
            dve.wait_ge(route, ROUTE0)
            dve.memset(keep[:, 0:NCH + 1:CB], 0.0).then_inc(route, 1)
            for m in restart:
                dve.memset(restart[m][:, 0:E * m:m], 0.0).then_inc(route, 1)
            ROUTE0 += 1 + len(restart)
            rc = [ROUTE0]

            def link(ins):
                rc[0] += 1
                ins.then_inc(route, 1)
                dve.wait_ge(route, rc[0])

            dve.wait_ge(pa_tanh, 1)
            prepared(dve.tensor_scalar(pa[:], pa[:], 0.5, 0.5, ALU.mult, ALU.add))
            dve.wait_ge(prep, 1)
            prepared(dve.tensor_tensor(q[:], pa[:, 0:2], pa[:, 2:4], ALU.mult))
            prepared(dve.tensor_tensor(cf[:], pa[:, 0:2], prm_sb[:, 4:6], ALU.mult))
            dve.wait_ge(prep, 3)
            prepared(dve.tensor_scalar(q[:], q[:], -1.0, 1.0, ALU.mult, ALU.add))
            prepared(dve.tensor_scalar(om[:], prm_sb[:, 8:9], 0.5, None, ALU.mult))
            prepared(dve.scalar_tensor_tensor(cf[:], cf[:], 0.5 * SCALE, prm_sb[:, 6:8], ALU.mult, ALU.mult))
            dve.wait_ge(const, 11)
            prepared(dve.tensor_scalar(centre[:], ident[:], -1.0 / D, None, ALU.add))
            dve.wait_ge(rwc_ps, 1)
            prepared(dve.tensor_copy(rwc[:], bank_a[:, 0:E]))
            dve.wait_ge(b_in, 32)
            prepared(dve.tensor_copy(bpart[:, 0, :], bcol[:]))
            dve.wait_ge(prep, 9)
            prepared(dve.tensor_tensor(bcol[:], bcol[:], bpart[:, 0, :], ALU.subtract))
            dve.wait_ge(prep, 10)
            prepared(dve.tensor_copy(bpart[:, 1, :], bcol[:]))
            dve.wait_ge(prep, 11)
            prepared(dve.tensor_tensor(bpart[:, 2, :], bcol[:], bpart[:, 1, :], ALU.subtract))
            dve.wait_ge(prep, PREP_DVE)
            assert steps[0] == PREP_DVE

            def mix_1(a):
                xc = x_sb[:, bass.ds(a * CH, CH)]
                dve.wait_ge(carry_ready, a + 1)
                for n, ready in ((0, h1_ready), (1, h2_ready)):
                    dve.tensor_tensor_scan(h[:, n, :], q[:, n:n + 1].to_broadcast([P, CH]), xc,
                                           carry[:, n:n + 1], ALU.mult, ALU.add).then_inc(ready, 1)
                dve.wait_ge(h2_ready, a + 1)
                dve.tensor_tensor(carry[:], h[:, :, CH - 1], keep[:, bass.ds(a + 1, 1)].to_broadcast([P, 2]),
                                  ALU.mult).then_inc(carry_ready, 1)
                dve.wait_ge(t1_ready, a + 1)
                dve.scalar_tensor_tensor(t2[:], h[:, 1, :], cf[:, 1:2], t1[:], ALU.mult, ALU.add)\
                    .then_inc(t2_ready, 1)
                dve.wait_ge(t2_ready, a + 1)
                dve.scalar_tensor_tensor(v[:], xc, om[:, 0:1], t2[:], ALU.mult, ALU.add).then_inc(v_ready, 1)

            def mix_2(a):
                xc = x_sb[:, bass.ds(a * CH, CH)]
                dve.wait_ge(th_ready, a + 1)
                dve.scalar_tensor_tensor(p[:], th[:], 1.0, v[:], ALU.add, ALU.mult).then_inc(p_ready, 1)
                dve.wait_ge(p_ready, a + 1)
                dve.tensor_tensor(s[:], p[:], xc, ALU.add).then_inc(s_ready, 1)

            def mix_3(a):
                dve.wait_ge(stok_ready, a + 1)
                for k in range(2):
                    last = dve.bn_stats(st_a[:, k, :], stok[:, k * P:(k + 1) * P])
                last.then_inc(st_ready, 1)
                dve.wait_ge(st_ready, a + 1)
                dve.memset(pace[:], 0.0)
                for k in range(2):
                    last = dve.bn_aggr(mv_a[:, k, :], st_a[:, k, :])
                last.then_inc(mv_ready, 1)
                dve.wait_ge(mv_ready, a + 1)
                dve.tensor_scalar(ve_a[:], mv_a[:, :, 1], LN_EPS, None, ALU.add).then_inc(ve_ready, 1)

            def mix_4(a):
                dve.wait_ge(rs_ready, a + 1)
                for k in range(2):
                    dve.tensor_scalar(logit[:, bass.ds(2 * a + k, 1), :].rearrange("p a e -> p (a e)"),
                                      raw[:, k * E:(k + 1) * E], rs_a[:, k:k + 1], None, ALU.mult)
                for k in range(2):
                    last = dve.tensor_scalar(x2[:, bass.ds(2 * a + k, 1), :].rearrange("p a e -> p (a e)"),
                                             stok[:, k * P:(k + 1) * P], mv_a[:, k, 0:1], rs_a[:, k:k + 1],
                                             ALU.subtract, ALU.mult)
                last.then_inc(x2_ready, 1)

            def route_group(gr):
                m, t0 = GROUPS[gr], T0[gr]
                full = [P, m, E]
                lg = logit[:, t0:t0 + m, :]
                o1, o2, wa, wk = (x[:, 0:m, :] for x in (oh[0], oh[1], ra, rk))
                revb = rev[:, :].rearrange("p (a e) -> p a e", a=1).to_broadcast(full)

                def over_e(x):
                    return x[:, 0:m].rearrange("p (t a) -> p t a", a=1).to_broadcast(full)

                def first_max(src, mx, o):
                    link(dve.tensor_reduce(mx[:, 0:m], src, AX.X, ALU.max))
                    link(dve.tensor_tensor(wk, src, over_e(mx), ALU.is_equal))
                    link(dve.tensor_tensor(wk, wk, revb, ALU.mult))
                    link(dve.tensor_reduce(rkm[:, 0:m], wk, AX.X, ALU.max))
                    link(dve.tensor_tensor(o, wk, over_e(rkm), ALU.is_equal))

                if gr == 0:
                    dve.wait_ge(row_in, 16)
                dve.wait_ge(x2_ready, (t0 + m) // 2)
                link(dve.tensor_tensor(lg, lg, rb.rearrange("p (a e) -> p a e", a=1).to_broadcast(full), ALU.add))
                first_max(lg, rm[0], o1)
                link(dve.tensor_scalar(wa, o1, -BIG, 0.5 * BIG, ALU.mult, ALU.add))
                link(dve.tensor_tensor(wa, wa, lg, ALU.min))
                first_max(wa, rm[1], o2)
                dve.tensor_tensor(rd[:, 0:m], rm[0][:, 0:m], rm[1][:, 0:m], ALU.subtract).then_inc(rd_ready, 1)
                dve.tensor_tensor(both[:, 0:m, :], o1, o2, ALU.add).then_inc(both_ready, 1)
                dve.wait_ge(counted, gr + 1)
                pos = bank_a[:, 0:m * E].rearrange("p (t e) -> p t e", e=E)
                totp = bank_a[:, P:P + m * E].rearrange("p (t e) -> p e t", e=E)
                totg = tot[:].rearrange("p e t -> p (e t)")[:, 0:E * m]
                incg = inc[:].rearrange("p e t -> p (e t)")[:, 0:E * m]
                tot3, inc3 = (x.rearrange("p (e t) -> p e t", t=m) for x in (totg, incg))
                link(dve.tensor_copy(tot3, totp))
                link(dve.tensor_tensor_scan(incg, restart[m][:], totg, 0.0, ALU.mult, ALU.add))
                fill3 = fill[:].rearrange("p e t -> p (e t)")[:, 0:E * m].rearrange("p (e t) -> p e t", t=m)
                link(dve.tensor_tensor(fill3, inc3[:, :, m - 1:m].to_broadcast([P, E, m]),
                                       k128[:, 0:m].rearrange("p (a t) -> p a t", a=1).to_broadcast([P, E, m]),
                                       ALU.is_gt))
                link(dve.tensor_reduce(nti[:], fill3, AX.X, ALU.add))
                link(dve.tensor_tensor_scan(ends[:], ones_e, nti[:], 0.0, ALU.mult, ALU.add))
                link(dve.tensor_tensor(base[:], ends[:], nti[:], ALU.subtract))
                link(dve.tensor_scalar(base[:], base[:], float(P), float(N0[gr] * P), ALU.mult, ALU.add))
                link(dve.tensor_tensor(inc3, inc3, tot3, ALU.subtract))
                link(dve.tensor_tensor(inc3, inc3, base[:].rearrange("p (e a) -> p e a", a=1)
                                       .to_broadcast([P, E, m]), ALU.add))
                link(dve.tensor_tensor(spos[:, 0:m, :], pos, inc3.rearrange("p e t -> p t e"), ALU.add))
                for k, o in enumerate((o1, o2)):
                    link(dve.tensor_tensor(wk, o, spos[:, 0:m, :], ALU.mult))
                    link(dve.tensor_reduce(slotf[:, k, 0:m], wk, AX.X, ALU.add))
                J = SLOTS[gr]
                link(dve.tensor_tensor(ecmp[0:1, 0:J, :],
                                       ends[0:1, :].rearrange("p (a e) -> p a e", a=1).to_broadcast([1, J, E]),
                                       jidx[0:1, 0:J].rearrange("p (j a) -> p j a", a=1).to_broadcast([1, J, E]),
                                       ALU.is_le))
                link(dve.tensor_reduce(esum[0:1, 0:J], ecmp[0:1, 0:J, :], AX.X, ALU.add))
                for n0 in (N0[gr], N0[gr] + 1):
                    j0, b, k = n0 - N0[gr], n0 // 2, n0 % 2
                    cnt = (J - j0 + 1) // 2
                    for row, col in ((b, 2 + k), (b + 1, k)):
                        dve.tensor_scalar(eid[0:1, row:row + cnt, col], esum[0:1, j0:J:2], float(E - 1), float(FF),
                                          ALU.min, ALU.mult)
                dve.tensor_copy(slots[:, :, t0:t0 + m], slotf[:, :, 0:m]).then_inc(slots_ready, 1)
                dve.wait_ge(rth_ready, gr + 1)
                dve.tensor_scalar(wts[:, 0, t0:t0 + m], rth[:, 0:m], 0.5, 0.5, ALU.mult, ALU.add)
                link(dve.tensor_scalar(wts[:, 1, t0:t0 + m], rth[:, 0:m], -0.5, 0.5, ALU.mult, ALU.add))

            ones_e = restart[min(restart)][:, 1:2].to_broadcast([P, E])

            def split_low():
                for k in range(2):
                    cols = slice(k * 2048, (k + 1) * 2048)
                    dve.wait_ge(whigh, k + 1)
                    dve.tensor_tensor(w1l[:, cols], stage[:, cols], w1h[:, cols].bitcast(f32), ALU.subtract)\
                        .then_inc(wlow, 1)

            def low_x(b):
                dve.wait_ge(xh_ready, b + 1)
                dve.tensor_tensor(xl[:], bank_x[:, 0:2 * P], xh[:].bitcast(f32), ALU.subtract).then_inc(xl_ready, 1)

            def close_1(d):
                dve.wait_ge(gathered, d + 1)
                src = [yg[:, bass.ds(d, 1), j, :].rearrange("p a e -> p (a e)") for j in range(4)]
                w = [[wts[:, top, bass.ds(2 * d + k, 1)] for top in range(2)] for k in range(2)]
                for k in range(2):
                    xk = x2[:, bass.ds(2 * d + k, 1), :].rearrange("p a e -> p (a e)")
                    last = dve.scalar_tensor_tensor(z[:, k, :], src[2 * k], w[k][0], xk, ALU.mult, ALU.add)
                last.then_inc(za_ready, 1)
                dve.wait_ge(za_ready, d + 1)
                for k in range(2):
                    last = dve.scalar_tensor_tensor(z[:, k, :], src[2 * k + 1], w[k][1], z[:, k, :], ALU.mult, ALU.add)
                last.then_inc(z_done, 1)
                stats(d, 0, z, z_done, dst_ready, dmv_ready, FFN_EPS, var1_ready)

            def stats(d, j, src, src_ready, st_sem, mv_sem, eps, var_sem):
                dve.wait_ge(src_ready, d + 1)
                for k in range(2):
                    last = dve.bn_stats(st_d[j][:, k, :], src[:, k, :])
                last.then_inc(st_sem, 1)
                dve.wait_ge(st_sem, d + 1)
                dve.memset(pace[:], 0.0)
                for k in range(2):
                    last = dve.bn_aggr(mv_d[j][:, k, :], st_d[j][:, k, :])
                last.then_inc(mv_sem, 1)
                dve.wait_ge(mv_sem, d + 1)
                dve.tensor_scalar(ve_d[j][:], mv_d[j][:, :, 1], eps, None, ALU.add).then_inc(var_sem, 1)

            def close_2(d):
                dve.wait_ge(rs1_ready, d + 1)
                for k in range(2):
                    last = dve.tensor_scalar(zn[:, k, :], z[:, k, :], mv_d[0][:, k, 0:1], rs_d[0][:, k:k + 1],
                                             ALU.subtract, ALU.mult)
                last.then_inc(zn_ready, 1)
                dve.wait_ge(zn_ready, d + 1)
                full = [P, 2, D]
                dve.tensor_tensor(zn[:], zn[:], lnw.rearrange("p (a e) -> p a e", a=1).to_broadcast(full),
                                  ALU.mult).then_inc(zw_ready, 1)
                dve.wait_ge(zw_ready, d + 1)
                dve.tensor_tensor(zn[:], zn[:], lnb.rearrange("p (a e) -> p a e", a=1).to_broadcast(full),
                                  ALU.add).then_inc(ub_ready, 1)
                dve.wait_ge(ub_ready, d + 1)
                dve.tensor_tensor(u[:], zn[:], x2[:, bass.ds(2 * d, 2), :], ALU.add).then_inc(u_ready, 1)
                stats(d, 1, u, u_ready, dst2_ready, dmv2_ready, LN_EPS, var2_ready)

            def close_3(d):
                dve.wait_ge(rs2_ready, d + 1)
                at_least(dve, o_out, 16 * d)
                for k in range(2):
                    last = dve.tensor_scalar(o_sb[:, k, :], u[:, k, :], mv_d[1][:, k, 0:1], rs_d[1][:, k:k + 1],
                                             ALU.subtract, ALU.mult)
                last.then_inc(o_ready, 1)

            def pair(b, before=None, behind=None):
                if before:
                    before()
                if not (isinstance(b, int) and b == PAIRS - 1):
                    low_x(b + 1)
                if behind:
                    behind()

            def close(d):
                begins = isinstance(d, int)
                if not (begins and d < 2):
                    close_3(d - 2)
                if not (begins and d < 1):
                    close_2(d - 1)
                close_1(d)

            for seg in SCHEDULE:
                kind = seg[0]
                if kind in ("A", "AC"):
                    a0 = seg[-1] if kind == "AC" else seg[1]
                    n = seg[2]
                    for k in range(4):
                        if a0 * CH <= k * SEQ < (a0 + n) * CH or (a0 * CH // SEQ == k):
                            dve.wait_ge(x_in[k], 16)

                    def body(i, kind=kind, a0=a0, b0=seg[1]):
                        begins = isinstance(i, int) and i == 0
                        a = a0 + i

                        def before_s():
                            if not begins:
                                mix_4(a - 1)
                            mix_2(a)
                        mix_1(a)
                        before_s()
                        if kind == "AC":
                            pair(b0 + i)
                        mix_3(a)
                    segment(dve, n, body)
                    mix_4(a0 + n - 1)
                elif kind == "R":
                    route_group(seg[1])
                    if seg[1] == 0:
                        split_low()
                    if seg[1] == 1:
                        low_x(0)
                elif kind == "C":
                    segment(dve, seg[2], lambda i, b0=seg[1]: pair(b0 + i), seg[1] + seg[2] == PAIRS)
                elif kind == "DC":
                    _, b0, n, d0 = seg
                    segment(dve, n, lambda i, b0=b0, d0=d0: pair(b0 + i, behind=lambda: close(d0 + i)),
                            b0 + n == PAIRS, first=2 if d0 == 0 else 1)
                else:
                    _, d0, n = seg
                    repeat(dve, d0, d0 + n, close)
                    close_3(NCH - 2)
                    close_2(NCH - 1)
                    close_3(NCH - 1)


_INS = ["xT", "prm", "rows", "rwT", "w1T", "w2T", "b1", "b2"]


def kernel(**inputs):
    import numpy as np
    import concourse.bacc as bacc
    from concourse.bass_utils import run_bass_kernel_spmd

    x = {k: np.asarray(v) for k, v in inputs.items()}
    x = {k.replace("L0_attn_", "").replace("L0_ffn_", ""): v for k, v in x.items()}
    laid = {
        "xT": x["x"].reshape(T, D).T,
        "prm": np.concatenate([x[k].reshape(D, -1) for k in ("delta", "alpha", "beta", "gamma", "omega")], axis=1),
        "rows": np.concatenate([x[k].reshape(1, -1) for k in ("router_b", "ln_w", "ln_b")], axis=1),
        "rwT": x["router_w"].T,
        "w1T": x["w1"].transpose(2, 0, 1).reshape(D, E * FF),
        "w2T": x["w2"].reshape(E, D, FC, P).transpose(3, 0, 2, 1).reshape(P, E * FF),
        "b1": x["b1"].reshape(P, E * FF // P),
        "b2": x["b2"].reshape(P, E * D // P),
    }
    nc = bacc.Bacc("TRN2", target_bir_lowering=False, num_devices=1)
    arrays, args = {}, []
    for name in _INS:
        a = np.ascontiguousarray(laid[name])
        arrays[f"in_{name}"] = a
        args.append(nc.dram_tensor(f"in_{name}", a.shape, mybir.dt.from_np(a.dtype), kind="ExternalInput").ap())
    args.append(nc.dram_tensor("out_0", (T, D), f32, kind="ExternalOutput").ap())
    ema_moe_kernel(nc, *args)
    r = run_bass_kernel_spmd(nc, [arrays], core_ids=[0])
    return r.results[0]["out_0"].reshape(BATCH, SEQ, D)
```

```python
import math
from contextlib import ExitStack

import concourse.bass as bass
from concourse import mybir

f32 = mybir.dt.float32
f32r = mybir.dt.float32r
bf16 = mybir.dt.bfloat16
i32 = mybir.dt.int32
ALU = mybir.AluOpType
ACT = mybir.ActivationFunctionType
AX = mybir.AxisListType

P = 128
BATCH, SEQ, D = 4, 1024, 128
T = BATCH * SEQ
E, FF, TOP = 8, 512, 2
FC = FF // P
CH = 2 * P
NCH = T // CH
NT = T // P
CB = SEQ // CH
SCALE = math.sqrt(0.5)
LN_EPS, FFN_EPS = 1e-5, 1e-12
BIG = 3.0e38

GROUPS = [4, 8, 14, 6]
G = len(GROUPS)
T0 = [sum(GROUPS[:g]) for g in range(G + 1)]
SLOTS = [TOP * m + E - 1 for m in GROUPS]
N0 = [sum(SLOTS[:g]) for g in range(G + 1)]
NS = N0[G]
PAIRS = NS // 2
assert T0[G] == NT and NS % 2 == 0 and all(m % 2 == 0 for m in GROUPS)

SCHEDULE = [
    ("A", 0, 2), ("R", 0), ("A", 2, 3),
    ("AC", 0, 1, 5), ("RC", 1, 1), ("AC", 3, 7, 6), ("RC", 2, 10), ("AC", 12, 3, 13), ("RC", 3, 15),
    ("C", 17, 7), ("DC", 24, 6, 0), ("C", 30, 9), ("DC", 39, 7, 6),
    ("D", 13),
]
POOL = [("a", 0), ("a", 1)] + [("w", k) for k in range(4)]
POOL += [("S", 0, 0, 3), ("a", 2), ("S", 0, 3, 3), ("a", 3), ("S", 0, 6, 2), ("a", 4), ("a", 5)]
POOL += [("S", 1, 0, 7), ("a", 6), ("S", 1, 7, 6), ("a", 7), ("S", 1, 13, 3)] + [("a", a) for a in range(8, 13)]
POOL += [("S", 2, 0, 6), ("a", 13), ("S", 2, 6, 4), ("a", 14), ("S", 2, 10, 5), ("a", 15), ("S", 2, 15, 13)]
POOL += [("g", 0), ("g", 1), ("S", 3, 0, 12)] + [("g", d) for d in range(2, 6)] + [("n", d) for d in range(6)]
POOL += [("p", d) for d in range(6)]
POOL += [("g", 6), ("g", 7), ("n", 6)]
for _d in range(6, 11):
    POOL += [("g", _d + 2), ("p", _d), ("n", _d + 1)]
POOL += [("p", 11), ("n", 12), ("p", 12), ("g", 13), ("g", 14), ("p", 13), ("g", 15)]
POOL += [("p", d) for d in range(14, 17)]

TAIL = SCHEDULE[-1][1]

PREP_DVE = 12
CONST = 11


def at_least(eng, sem, value):
    if not (isinstance(value, int) and value <= 0):
        eng.wait_ge(sem, value)


def repeat(eng, lo, hi, body):
    if hi - lo <= 1:
        for i in range(lo, hi):
            body(i)
    else:
        with eng.Fori(lo, hi) as i:
            body(i)


def segment(eng, n, body, last_apart=False, first=1):
    for i in range(min(first, n)):
        body(i)
    hi = n - 1 if last_apart and n > 1 else n
    repeat(eng, first, hi, body)
    if hi < n:
        body(n - 1)


def ema_moe_kernel(nc, xT, prm, rows, rwT, w1T, w2T, b1, b2, out):
    xs_dram = nc.dram_tensor("slots_in", [NS * P, D], f32).ap()
    y_dram = nc.dram_tensor("slots_out", [NS * P, D], f32).ap()
    bias_dram = nc.dram_tensor("bias_parts", [3, E * FF + E * D], bf16).ap()

    ctx = ExitStack()
    with ctx:
        def sb(name, shape, dt=f32):
            return ctx.enter_context(nc.sbuf_tensor(name, shape, dt))

        def sem(name):
            return ctx.enter_context(nc.semaphore(name))

        x_sb = sb("x_sb", [P, T])
        x2 = sb("x2", [P, NT, D])
        w1h, w1l = sb("w1h", [P, E * FF], f32r), sb("w1l", [P, E * FF], f32r)
        w2 = sb("w2", [P, E * FF])
        yg = sb("yg", [P, NCH, 2 * TOP, D])
        stage = yg[:, :, :, :].rearrange("p a b c -> p (a b c)")
        bias = sb("bias", [P, 2, E, FF], bf16)
        b1_rows, b2_rows = (bias[:, k].rearrange("p e f -> p (e f)") for k in range(2))
        bcol = sb("bcol", [P, 40])
        bpart = sb("bpart", [P, 3, 40], bf16)
        prm_sb = sb("prm_sb", [P, 9])
        row_sb = sb("row_sb", [P, E + 2 * D])
        rb, lnw, lnb = row_sb[:, 0:E], row_sb[:, E:E + D], row_sb[:, E + D:E + 2 * D]
        rw_sb, rwc = sb("rw_sb", [P, E]), sb("rwc", [P, E])
        zeros = sb("zeros", [P, 8 * D])
        ident, centre = sb("ident", [P, P]), sb("centre", [P, P])
        ones, before = sb("ones", [P, P], bf16), sb("before", [P, P], bf16)
        power = sb("power", [P, 4])
        pa, q, cf, om = sb("pa", [P, 4]), sb("q", [P, 2]), sb("cf", [P, 2]), sb("om", [P, 1])
        keep = sb("keep", [P, NCH + 1])
        carry = sb("carry", [P, 2])
        h = sb("h", [P, 2, CH])
        t1, t2, v, th, p, s = (sb(n, [P, CH]) for n in ("t1", "t2", "v", "th", "p", "s"))
        st_a, mv_a, ve_a, rs_a = sb("st_a", [P, 2, 6]), sb("mv_a", [P, 2, 2]), sb("ve_a", [P, 2]), sb("rs_a", [P, 2])
        M = max(GROUPS)
        logit = sb("logit", [P, NT, E])
        oh = [sb("oh1", [P, M, E]), sb("oh2", [P, M, E])]
        ra, rk = sb("ra", [P, M, E]), sb("rk", [P, M, E])
        rm = [sb("rm1", [P, M]), sb("rm2", [P, M])]
        rkm, rd, rth = sb("rkm", [P, M]), sb("rd", [P, M]), sb("rth", [P, M])
        both = sb("both", [P, M, E], bf16)
        tot, inc = sb("tot", [P, E, M]), sb("inc", [P, E, M])
        nti, ends, base = sb("nti", [P, E]), sb("ends", [P, E]), sb("base", [P, E])
        fill = sb("fill", [P, E, M])
        spos = sb("spos", [P, M, E])
        slotf = sb("slotf", [P, TOP, M])
        slots = sb("slots", [P, TOP, NT], i32)
        wts = sb("wts", [P, TOP, NT])
        rev = sb("rev", [P, E])
        k128 = sb("k128", [P, M])
        restart = {m: sb(f"restart{m}", [P, E * m]) for m in sorted(set(GROUPS))}
        JM = max(SLOTS)
        jidx, ecmp, esum = sb("jidx", [1, JM]), sb("ecmp", [1, JM, E]), sb("esum", [1, JM])
        eid = sb("eid", [1, PAIRS + 1, 4], i32)
        xs = sb("xs", [P, 2, D])
        xh, xl = sb("xh", [P, 2 * P], f32r), sb("xl", [P, 2 * P], f32r)
        g = [sb(f"g{k}", [P, FF]) for k in range(2)]
        gt = [sb(f"gt{k}", [P, FF]) for k in range(2)]
        y_sb = sb("y_sb", [P, 2, D])
        z, zn, u = sb("z", [P, 2, D]), sb("zn", [P, 2, D]), sb("u", [P, 2, D])
        xb = sb("xb", [P, 2, D])
        o_sb = sb("o_sb", [P, 2, D])
        st_d, mv_d, ve_d, rs_d = sb("st_d", [P, 4, 6]), sb("mv_d", [P, 4, 2]), sb("ve_d", [P, 4]), sb("rs_d", [P, 4])

        def pb(name):
            return ctx.enter_context(nc.psum_tensor(name, [P, 512], f32))

        bank_a, bank_x = pb("bank_a"), pb("bank_x")
        bank_z = [pb(f"bank_z{k}") for k in range(2)]
        bank_g = [pb(f"bank_g{k}") for k in range(2)]
        bank_y = [pb(f"bank_y{k}") for k in range(2)]
        pace = sb("pace", [P, 1])
        stok = bank_a[:, 0:CH]
        raw = bank_a[:, CH:CH + 2 * E]

        prm_in, row_in, rw_in, b_in = sem("prm_in"), sem("row_in"), sem("rw_in"), sem("b_in")
        x_in = [sem(f"x_in{k}") for k in range(4)]
        w_in = [sem(f"w_in{k}") for k in range(4)]
        bias_out, bias_back = sem("bias_out"), sem("bias_back")
        cleared = [sem(f"cleared{k}") for k in range(G)]
        const = sem("const")
        pa_tanh = sem("pa_tanh")
        prep = sem("prep")
        rwc_ps = sem("rwc_ps")
        whigh, wlow = sem("whigh"), sem("wlow")
        h1_ready, h2_ready, carry_ready = sem("h1_ready"), sem("h2_ready"), sem("carry_ready")
        t1_ready, t2_ready, v_ready, th_ready = sem("t1_ready"), sem("t2_ready"), sem("v_ready"), sem("th_ready")
        p_ready, s_ready, stok_ready = sem("p_ready"), sem("s_ready"), sem("stok_ready")
        st_ready, mv_ready, ve_ready, rs_ready = sem("st_ready"), sem("mv_ready"), sem("ve_ready"), sem("rs_ready")
        x2_ready = sem("x2_ready")
        route = sem("route")
        both_ready, counted, rd_ready, rth_ready = sem("both_ready"), sem("counted"), sem("rd_ready"), sem("rth_ready")
        slots_ready, experts_ready = sem("slots_ready"), sem("experts_ready")
        scattered = [sem(f"scattered{k}") for k in range(G)]
        xs_in, xsT_ready, xh_ready, xl_ready = sem("xs_in"), sem("xsT_ready"), sem("xh_ready"), sem("xl_ready")
        z_ready, g_ready, gT_ready = sem("z_ready"), sem("g_ready"), sem("gT_ready")
        gt_ready, y_ready, y_moved = sem("gt_ready"), sem("y_ready"), sem("y_moved")
        y_out = sem("y_out")
        gathering = [sem(f"gathering{k}") for k in range(2)]
        gathered = sem("gathered")
        za_ready, z_done, dst_ready = sem("za_ready"), sem("z_done"), sem("dst_ready")
        dmv_ready, dvar_ready, drs_ready = sem("dmv_ready"), sem("dvar_ready"), sem("drs_ready")
        zn_ready, xb_ready, u_ready = sem("zn_ready"), sem("xb_ready"), sem("u_ready")
        o_ready, o_out = sem("o_ready"), sem("o_out")

        block = ctx.enter_context(nc.Block())

        @block.sync
        def _(sp):
            sp.dma_start(prm_sb[:], prm).then_inc(prm_in, 16)
            XP = T // 4
            sp.dma_start(x_sb[:, 0:XP], xT[:, 0:XP]).then_inc(x_in[0], 16)
            sp.dma_start(rw_sb[:], rwT).then_inc(rw_in, 16)
            sp.dma_start(row_sb[:], rows.to_broadcast([P, E + 2 * D])).then_inc(row_in, 16)
            sp.dma_start(bcol[:, 0:32], b1).then_inc(b_in, 16)
            sp.dma_start(bcol[:, 32:40], b2).then_inc(b_in, 16)

            def clear(gr):
                for n in range(N0[gr], N0[gr + 1], 8):
                    k = min(8, N0[gr + 1] - n)
                    sp.dma_start(xs_dram[n * P:(n + k) * P, :].rearrange("(p r) d -> p (r d)", p=P),
                                 zeros[:, 0:k * D]).then_inc(cleared[gr], 16)

            sp.wait_ge(const, 1)
            clear(0)
            for k in range(2):
                cols = slice(k * 2048, (k + 1) * 2048)
                sp.dma_start(stage[:, cols], w1T[:, cols]).then_inc(w_in[k], 16)
            sp.dma_start(x_sb[:, XP:2 * XP], xT[:, XP:2 * XP]).then_inc(x_in[1], 16)
            sp.wait_ge(prep, PREP_DVE)
            for r in range(3):
                sp.dma_start(bias_dram[r, 0:E * FF].rearrange("(p c) -> p c", p=P),
                             bpart[:, r, 0:32]).then_inc(bias_out, 16)
                sp.dma_start(bias_dram[r, E * FF:].rearrange("(p c) -> p c", p=P),
                             bpart[:, r, 32:40]).then_inc(bias_out, 16)
            for k in range(2):
                cols = slice(k * 2048, (k + 1) * 2048)
                sp.dma_start(w2[:, cols], w2T[:, cols]).then_inc(w_in[2 + k], 16)
            sp.wait_ge(bias_out, 6 * 16)
            sp.wait_ge(const, CONST)
            sp.dma_start(b1_rows[0:3, :], bias_dram[:, 0:E * FF]).then_inc(bias_back, 16)
            sp.dma_start(bias[0:3, 1, :, 0:D], bias_dram[:, E * FF:].rearrange("r (e d) -> r e d", e=E))\
                .then_inc(bias_back, 16)
            for k in range(2, 4):
                sp.dma_start(x_sb[:, k * XP:(k + 1) * XP], xT[:, k * XP:(k + 1) * XP]).then_inc(x_in[k], 16)
            for gr in range(1, G):
                clear(gr)

            def load(b):
                at_least(sp, xsT_ready, b)
                sp.dma_start(xs[:], xs_dram[bass.ds(b * 2 * P, 2 * P), :].rearrange("(k p) d -> p k d", p=P))\
                    .then_inc(xs_in, 16)

            def store_y(b):
                sp.wait_ge(y_moved, 2 * b + 2)
                sp.dma_start(y_dram[bass.ds(b * 2 * P, 2 * P), :].rearrange("(k p) d -> p k d", p=P), y_sb[:])\
                    .then_inc(y_out, 16)

            def store_o(d):
                sp.wait_ge(o_ready, d + 1)
                sp.dma_start(out[bass.ds(d * CH, CH), :].rearrange("(k p) d -> p k d", p=P), o_sb[:])\
                    .then_inc(o_out, 16)

            def group_wait(b):
                for k in range(G):
                    if N0[k] // 2 == b:
                        sp.wait_ge(scattered[k], 16 * TOP * GROUPS[k])

            first_of = [N0[k] // 2 for k in range(G)]

            def pairs(b0, n, d0=None):
                at = b0
                while at < b0 + n:
                    if at + 2 in first_of and at + 2 < PAIRS:
                        group_wait(at + 2)
                    end = at + 1
                    while end < b0 + n and end + 2 not in first_of and (end + 2 < PAIRS) == (at + 2 < PAIRS) \
                            and at >= 1 and (d0 != 0 or at >= b0 + 2):
                        end += 1

                    def body(b, at=at):
                        if at + 2 < PAIRS:
                            load(b + 2)
                        if at >= 1:
                            store_y(b - 1)
                        if d0 is not None and not (d0 == 0 and at < b0 + 2):
                            store_o(b - b0 + d0 - 2)
                    repeat(sp, at, end, body)
                    at = end

            group_wait(0)
            load(0)
            load(1)
            for seg in SCHEDULE:
                if seg[0] in ("C", "AC"):
                    pairs(seg[1], seg[2])
                elif seg[0] == "RC":
                    pairs(seg[2], 2)
                elif seg[0] == "DC":
                    _, b0, n, d0 = seg
                    pairs(b0, n, d0)
                    if b0 + n == PAIRS:
                        store_y(PAIRS - 1)
                elif seg[0] == "D":
                    repeat(sp, seg[1] - 2, NCH, store_o)
            sp.wait_ge(o_out, 16 * NCH)

        @block.gpsimd
        def _(pool):
            pool.memset(zeros[:], 0.0).then_inc(const, 1)
            pool.memset(ident[:], 0.0).then_inc(const, 1)
            pool.memset(ones[:], 1.0).then_inc(const, 1)
            pool.wait_ge(const, 3)
            pool.affine_select(out=ident[:], in_=ident[:], compare_op=ALU.not_equal, fill=1.0, base=0,
                               pattern=[[-1, P]], channel_multiplier=1).then_inc(const, 1)
            pool.affine_select(out=before[:], in_=ones[:], compare_op=ALU.is_gt, fill=0.0, base=0,
                               pattern=[[1, P]], channel_multiplier=-1).then_inc(const, 1)
            pool.memset(power[:], -0.5).then_inc(const, 1)
            imprecise = dict(channel_multiplier=0, allow_small_or_imprecise_dtypes=True)
            pool.iota(rev[:], pattern=[[-1, E]], base=E, **imprecise).then_inc(const, 1)
            pool.iota(k128[:], pattern=[[P, M]], base=0, **imprecise).then_inc(const, 1)
            pool.iota(jidx[:], pattern=[[1, JM]], base=0, **imprecise).then_inc(const, 1)
            pool.memset(b1_rows, 0.0).then_inc(const, 1)
            pool.memset(bias[:, 1, :, 0:D], 0.0).then_inc(const, 1)

            def scatter(gr, k0, n):
                if k0 == 0:
                    pool.wait_ge(slots_ready, gr + 1)
                    pool.wait_ge(cleared[gr], 16 * -(-SLOTS[gr] // 8))
                for k in range(k0, k0 + n):
                    t, top = T0[gr] + k // TOP, k % TOP
                    pool.indirect_dma_start(
                        out=xs_dram, out_offset=bass.IndirectOffsetOnAxis(ap=slots[:, top, t:t + 1], axis=0),
                        in_=x2[:, t, :], in_offset=None, bounds_check=NS * P - 1, oob_is_err=False,
                    ).then_inc(scattered[gr], 16)

            def gather(d):
                written = next(N0[gr + 1] * P for gr in range(G) if 2 * d < T0[gr + 1])
                for gr in range(G):
                    if 2 * d == T0[gr]:
                        pool.wait_ge(y_out, 16 * ((N0[gr + 1] - 1) // 2 + 1))
                if d >= 2:
                    pool.wait_ge(gathering[d % 2], 64 * (d // 2))
                for k in range(2):
                    for top in range(TOP):
                        pool.indirect_dma_start(
                            out=yg[:, d, 2 * k + top, :], out_offset=None, in_=y_dram[0:written, :],
                            in_offset=bass.IndirectOffsetOnAxis(ap=slots[:, top, 2 * d + k:2 * d + k + 1], axis=0),
                            bounds_check=written - 1, oob_is_err=False,
                        ).then_inc(gathering[d % 2], 16)

            def split_low(k):
                cols = slice(k * 1024, (k + 1) * 1024)
                pool.wait_ge(whigh, k // 2 + 1)
                pool.tensor_tensor(w1l[:, cols], stage[:, cols], w1h[:, cols].bitcast(f32), ALU.subtract)\
                    .then_inc(wlow, 1)

            for item in POOL:
                kind, d = item[0], item[1]
                if kind == "w":
                    split_low(d)
                    continue
                if kind == "a":
                    pool.wait_ge(ve_ready, d + 1)
                    pool.tensor_tensor(rs_a[:], ve_a[:], power[:, 0:2], ALU.pow).then_inc(rs_ready, 1)
                elif kind == "S":
                    scatter(*item[1:])
                elif kind == "g":
                    gather(d)
                elif kind == "n":
                    pool.wait_ge(gathering[d % 2], 64 * (d // 2 + 1))
                    pool.engine_nop().then_inc(gathered, 1)
                else:
                    pool.wait_ge(dvar_ready, d + 1)
                    pool.tensor_tensor(rs_d[:], ve_d[:], power[:], ALU.pow).then_inc(drs_ready, 1)

        @block.scalar
        def _(act):
            act.wait_ge(prm_in, 16)
            act.activation(pa[:], prm_sb[:, 0:4], ACT.Tanh, scale=0.5).then_inc(pa_tanh, 1)

            def split_high():
                for k in range(2):
                    cols = slice(k * 2048, (k + 1) * 2048)
                    act.wait_ge(w_in[k], 16)
                    act.activation(w1h[:, cols], stage[:, cols], ACT.Copy).then_inc(whigh, 1)

            def scale_h1(a):
                act.wait_ge(h1_ready, a + 1)
                if isinstance(a, int) and a == 0:
                    act.wait_ge(prep, 6)
                else:
                    act.wait_ge(t2_ready, a)
                act.activation(t1[:], h[:, 0, :], ACT.Copy, scale=cf[:, 0:1]).then_inc(t1_ready, 1)

            def tanh_v(a):
                act.wait_ge(v_ready, a + 1)
                at_least(act, p_ready, a)
                act.activation(th[:], v[:], ACT.Tanh).then_inc(th_ready, 1)

            def high_x(b):
                act.wait_ge(xsT_ready, b + 1)
                act.activation(xh[:], bank_x[:, 0:2 * P], ACT.Copy).then_inc(xh_ready, 1)

            def gelu(n, k):
                act.wait_ge(z_ready, n + 1)
                act.activation(g[k][:], bank_z[k][:], ACT.Gelu).then_inc(g_ready, 1)

            def move_g(n, k):
                act.wait_ge(gT_ready, n + 1)
                act.activation(gt[k][:], bank_g[k][:], ACT.Copy).then_inc(gt_ready, 1)

            def move_y(n, k, first=False):
                act.wait_ge(y_ready, n + 1)
                if k == 0 and not first:
                    act.wait_ge(y_out, 8 * n)
                act.activation(y_sb[:, k, :], bank_y[k][:, 0:D], ACT.Copy).then_inc(y_moved, 1)

            def pair(b, a=None):
                first, last = isinstance(b, int) and b == 0, isinstance(b, int) and b == PAIRS - 1
                if isinstance(a, int) and a == NCH:
                    a = None
                gelu(2 * b, 0)
                if not first:
                    move_g(2 * b - 1, 1)
                if a is not None:
                    scale_h1(a)
                if not last:
                    high_x(b + 1)
                gelu(2 * b + 1, 1)
                move_g(2 * b, 0)
                if a is not None:
                    tanh_v(a)
                if not first:
                    move_y(2 * b - 2, 0, first=isinstance(b, int) and b == 1)
                    move_y(2 * b - 1, 1)

            groups_routed = 0
            for seg in SCHEDULE:
                kind = seg[0]
                if kind == "A":
                    if seg[1] == 0:
                        scale_h1(0)
                        tanh_v(0)
                    repeat(act, seg[1] + 1, seg[1] + seg[2] + 1, lambda a: (scale_h1(a), tanh_v(a)))
                elif kind in ("R", "RC"):
                    gr = seg[1]
                    if kind == "RC":
                        pair(seg[2])
                        pair(seg[2] + 1)
                    if gr == 0:
                        split_high()
                    act.wait_ge(rd_ready, gr + 1)
                    act.activation(rth[:, 0:GROUPS[gr]], rd[:, 0:GROUPS[gr]], ACT.Tanh, scale=0.5)\
                        .then_inc(rth_ready, 1)
                elif kind == "AC":
                    _, b0, n, a0 = seg
                    if b0 == 0:
                        high_x(0)
                    segment(act, n, lambda i, b0=b0, a0=a0: pair(b0 + i, a0 + i + 1), a0 + n == NCH,
                            first=2 if b0 == 0 else 1)
                elif kind == "C":
                    segment(act, seg[2], lambda i, b0=seg[1]: pair(b0 + i), seg[1] + seg[2] == PAIRS)
                elif kind == "DC":
                    _, b0, n, d0 = seg
                    segment(act, n, lambda i, b0=b0: pair(b0 + i), b0 + n == PAIRS)
                    if b0 + n == PAIRS:
                        move_g(NS - 1, 1)
                        move_y(NS - 2, 0)
                        move_y(NS - 1, 1)

        @block.tensor
        def _(pe):
            pe.wait_ge(prep, 7)
            pe.wait_ge(rw_in, 16)
            pe.matmul(bank_a[:, 0:E], centre[:], rw_sb[:], start=True, stop=True).then_inc(rwc_ps, 1)
            pe.wait_ge(prep, 8)

            def turn_s(a):
                pe.wait_ge(s_ready, a + 1)
                at_least(pe, x2_ready, a)
                for k in range(2):
                    pe.transpose(stok[:, k * P:(k + 1) * P], s[:, k * P:(k + 1) * P], ident[:])
                for k in range(2):
                    last = pe.matmul(raw[:, k * E:(k + 1) * E], s[:, k * P:(k + 1) * P], rwc[:], start=True, stop=True)
                last.then_inc(stok_ready, 1)

            def turn_x(b):
                pe.wait_ge(xs_in, 16 * (b + 1))
                at_least(pe, xl_ready, b)
                for k in range(2):
                    last = pe.transpose(bank_x[:, k * P:(k + 1) * P], xs[:, k, :], ident[:])
                last.then_inc(xsT_ready, 1)

            def experts(b):
                _, values = nc.values_load_multi_w_load_instructions(
                    eid[0:1, bass.ds(b, 1), :], engines=[mybir.EngineType.PE], min_val=0, max_val=(E - 1) * FF,
                    skip_runtime_bounds_check_because="counts of experts, kept to E - 1 by a minimum on the chip")
                return values

            def up(b, k, e):
                cols = bass.ds(e, FF)
                if k == 0:
                    pe.wait_ge(xl_ready, b + 1)
                at_least(pe, g_ready, 2 * b + k - 1)
                xhk, xlk = xh[:, k * P:(k + 1) * P], xl[:, k * P:(k + 1) * P]
                zb = bank_z[k][:]
                pe.matmul(zb, xhk, w1h[:, cols], start=True, stop=False)
                pe.matmul(zb, xhk, w1l[:, cols], start=False, stop=False)
                pe.matmul(zb, xlk, w1h[:, cols], start=False, stop=False)
                pe.matmul(zb, ones[:], b1_rows[:, cols], start=False, stop=True).then_inc(z_ready, 1)

            def turn_g(n, k):
                pe.wait_ge(g_ready, n + 1)
                at_least(pe, gt_ready, n - 1)
                for c in range(FC):
                    last = pe.transpose(bank_g[k][:, c * P:(c + 1) * P], g[k][:, c * P:(c + 1) * P], ident[:])
                last.then_inc(gT_ready, 1)

            def down(n, k, e):
                pe.wait_ge(gt_ready, n + 1)
                at_least(pe, y_moved, n - 1)
                yb = bank_y[k][:, 0:D]
                for c in range(FC):
                    pe.matmul(yb, gt[k][:, c * P:(c + 1) * P], w2[:, bass.ds(e + c * P, P)],
                              start=(c == 0), stop=False)
                pe.matmul(yb, ones[:], b2_rows[:, bass.ds(e, D)], start=False, stop=True)\
                    .then_inc(y_ready, 1)

            def pair(b, a=None):
                first, last = isinstance(b, int) and b == 0, isinstance(b, int) and b == PAIRS - 1
                before0, before1, own0, own1 = experts(b)
                up(b, 0, own0)
                if not first:
                    turn_g(2 * b - 1, 1)
                    down(2 * b - 2, 0, before0)
                up(b, 1, own1)
                if not last:
                    turn_x(b + 1)
                turn_g(2 * b, 0)
                if not first:
                    down(2 * b - 1, 1, before1)
                if a is not None:
                    turn_s(a)

            for seg in SCHEDULE:
                kind = seg[0]
                if kind in ("AC", "C", "DC", "RC"):
                    b0, end = (seg[2], seg[2] + 2) if kind == "RC" else (seg[1], seg[1] + seg[2])
                    for gr in range(G):
                        if b0 <= N0[gr] // 2 < end:
                            pe.wait_ge(experts_ready, gr + 1)
                if kind == "A":
                    segment(pe, seg[2], lambda i, a0=seg[1]: turn_s(a0 + i))
                elif kind in ("R", "RC"):
                    gr = seg[1]
                    m = GROUPS[gr]
                    if kind == "RC":
                        pair(seg[2])
                    pe.wait_ge(both_ready, gr + 1)
                    pe.wait_ge(x2_ready, T0[gr + 1] // 2)
                    mm = both[:].rearrange("p t e -> p (t e)")[:, 0:m * E]
                    pe.matmul(bank_a[:, 0:m * E], before[:], mm, start=True, stop=True)
                    pe.matmul(bank_a[:, P:P + m * E], ones[:], mm, start=True, stop=True).then_inc(counted, 1)
                    if kind == "RC":
                        pair(seg[2] + 1)
                    pe.wait_ge(slots_ready, gr + 1)
                elif kind == "AC":
                    _, b0, n, a0 = seg
                    if b0 == 0:
                        turn_x(0)
                        pe.wait_ge(wlow, 4)
                        for k in range(2, 4):
                            pe.wait_ge(w_in[k], 16)
                        pe.wait_ge(bias_back, 32)
                    segment(pe, n, lambda i, b0=b0, a0=a0: pair(b0 + i, a0 + i), first=2 if b0 == 0 else 1)
                elif kind == "C":
                    segment(pe, seg[2], lambda i, b0=seg[1]: pair(b0 + i), seg[1] + seg[2] == PAIRS)
                elif kind == "DC":
                    _, b0, n, d0 = seg
                    segment(pe, n, lambda i, b0=b0: pair(b0 + i), b0 + n == PAIRS)
                    if b0 + n == PAIRS:
                        turn_g(NS - 1, 1)
                        before0, before1, _, _ = experts(PAIRS)
                        down(NS - 2, 0, before0)
                        down(NS - 1, 1, before1)

        @block.vector
        def _(dve):
            steps = [0]

            def prepared(ins):
                ins.then_inc(prep, 1)
                steps[0] += 1

            dve.memset(carry[:], 0.0).then_inc(carry_ready, 1)
            dve.memset(keep[:], 1.0).then_inc(route, 1)
            dve.memset(ve_d[:], 1.0).then_inc(route, 1)
            dve.memset(eid[:], 0).then_inc(route, 1)
            for m in restart:
                dve.memset(restart[m][:], 1.0).then_inc(route, 1)
            ROUTE0 = 3 + len(restart)
            dve.wait_ge(route, ROUTE0)
            dve.memset(keep[:, 0:NCH + 1:CB], 0.0).then_inc(route, 1)
            for m in restart:
                dve.memset(restart[m][:, 0:E * m:m], 0.0).then_inc(route, 1)
            ROUTE0 += 1 + len(restart)
            rc = [ROUTE0]

            def link(ins, wait=True):
                rc[0] += 1
                ins.then_inc(route, 1)
                if wait:
                    dve.wait_ge(route, rc[0])

            dve.wait_ge(pa_tanh, 1)
            prepared(dve.tensor_scalar(pa[:], pa[:], 0.5, 0.5, ALU.mult, ALU.add))
            dve.wait_ge(prep, 1)
            prepared(dve.tensor_tensor(q[:], pa[:, 0:2], pa[:, 2:4], ALU.mult))
            prepared(dve.tensor_tensor(cf[:], pa[:, 0:2], prm_sb[:, 4:6], ALU.mult))
            dve.wait_ge(prep, 3)
            prepared(dve.tensor_scalar(q[:], q[:], -1.0, 1.0, ALU.mult, ALU.add))
            prepared(dve.tensor_scalar(om[:], prm_sb[:, 8:9], 0.5, None, ALU.mult))
            prepared(dve.scalar_tensor_tensor(cf[:], cf[:], 0.5 * SCALE, prm_sb[:, 6:8], ALU.mult, ALU.mult))
            dve.wait_ge(const, 9)
            prepared(dve.tensor_scalar(centre[:], ident[:], -1.0 / D, None, ALU.add))
            dve.wait_ge(rwc_ps, 1)
            prepared(dve.tensor_copy(rwc[:], bank_a[:, 0:E]))
            dve.wait_ge(b_in, 32)
            prepared(dve.tensor_copy(bpart[:, 0, :], bcol[:]))
            dve.wait_ge(prep, 9)
            prepared(dve.tensor_tensor(bcol[:], bcol[:], bpart[:, 0, :], ALU.subtract))
            dve.wait_ge(prep, 10)
            prepared(dve.tensor_copy(bpart[:, 1, :], bcol[:]))
            dve.wait_ge(prep, 11)
            prepared(dve.tensor_tensor(bpart[:, 2, :], bcol[:], bpart[:, 1, :], ALU.subtract))
            dve.wait_ge(prep, PREP_DVE)
            assert steps[0] == PREP_DVE

            def mix_1(a):
                xc = x_sb[:, bass.ds(a * CH, CH)]
                dve.wait_ge(carry_ready, a + 1)
                for n, ready in ((0, h1_ready), (1, h2_ready)):
                    dve.tensor_tensor_scan(h[:, n, :], q[:, n:n + 1].to_broadcast([P, CH]), xc,
                                           carry[:, n:n + 1], ALU.mult, ALU.add).then_inc(ready, 1)
                dve.wait_ge(h2_ready, a + 1)
                dve.tensor_tensor(carry[:], h[:, :, CH - 1], keep[:, bass.ds(a + 1, 1)].to_broadcast([P, 2]),
                                  ALU.mult).then_inc(carry_ready, 1)

            def mix_v(a):
                xc = x_sb[:, bass.ds(a * CH, CH)]
                dve.wait_ge(t1_ready, a + 1)
                dve.scalar_tensor_tensor(t2[:], h[:, 1, :], cf[:, 1:2], t1[:], ALU.mult, ALU.add)\
                    .then_inc(t2_ready, 1)
                dve.wait_ge(t2_ready, a + 1)
                dve.scalar_tensor_tensor(v[:], xc, om[:, 0:1], t2[:], ALU.mult, ALU.add).then_inc(v_ready, 1)

            def mix_2(a):
                xc = x_sb[:, bass.ds(a * CH, CH)]
                dve.wait_ge(th_ready, a + 1)
                dve.scalar_tensor_tensor(p[:], th[:], 1.0, v[:], ALU.add, ALU.mult).then_inc(p_ready, 1)
                dve.wait_ge(p_ready, a + 1)
                dve.tensor_tensor(s[:], p[:], xc, ALU.add).then_inc(s_ready, 1)

            def mix_3(a):
                dve.wait_ge(stok_ready, a + 1)
                for k in range(2):
                    last = dve.bn_stats(st_a[:, k, :], stok[:, k * P:(k + 1) * P])
                last.then_inc(st_ready, 1)
                dve.wait_ge(st_ready, a + 1)
                dve.memset(pace[:], 0.0)
                for k in range(2):
                    last = dve.bn_aggr(mv_a[:, k, :], st_a[:, k, :])
                last.then_inc(mv_ready, 1)
                dve.wait_ge(mv_ready, a + 1)
                dve.tensor_scalar(ve_a[:], mv_a[:, :, 1], LN_EPS, None, ALU.add).then_inc(ve_ready, 1)

            def mix_4(a):
                dve.wait_ge(rs_ready, a + 1)
                for k in range(2):
                    dve.tensor_scalar(logit[:, bass.ds(2 * a + k, 1), :].rearrange("p a e -> p (a e)"),
                                      raw[:, k * E:(k + 1) * E], rs_a[:, k:k + 1], None, ALU.mult)
                for k in range(2):
                    last = dve.tensor_scalar(x2[:, bass.ds(2 * a + k, 1), :].rearrange("p a e -> p (a e)"),
                                             stok[:, k * P:(k + 1) * P], mv_a[:, k, 0:1], rs_a[:, k:k + 1],
                                             ALU.subtract, ALU.mult)
                last.then_inc(x2_ready, 1)

            def route_group(gr, beside=None):
                m, t0 = GROUPS[gr], T0[gr]
                full = [P, m, E]
                lg = logit[:, t0:t0 + m, :]
                o1, o2, wa, wk = (x[:, 0:m, :] for x in (oh[0], oh[1], ra, rk))
                revb = rev[:, :].rearrange("p (a e) -> p a e", a=1).to_broadcast(full)

                def over_e(x):
                    return x[:, 0:m].rearrange("p (t a) -> p t a", a=1).to_broadcast(full)

                def first_max(src, mx, o):
                    link(dve.tensor_reduce(mx[:, 0:m], src, AX.X, ALU.max))
                    link(dve.tensor_tensor(wk, src, over_e(mx), ALU.is_equal))
                    link(dve.tensor_tensor(wk, wk, revb, ALU.mult))
                    link(dve.tensor_reduce(rkm[:, 0:m], wk, AX.X, ALU.max))
                    link(dve.tensor_tensor(o, wk, over_e(rkm), ALU.is_equal))

                if gr == 0:
                    dve.wait_ge(row_in, 16)
                dve.wait_ge(x2_ready, (t0 + m) // 2)
                link(dve.tensor_tensor(lg, lg, rb.rearrange("p (a e) -> p a e", a=1).to_broadcast(full), ALU.add))
                first_max(lg, rm[0], o1)
                link(dve.tensor_scalar(wa, o1, -BIG, 0.5 * BIG, ALU.mult, ALU.add))
                link(dve.tensor_tensor(wa, wa, lg, ALU.min))
                first_max(wa, rm[1], o2)
                dve.tensor_tensor(rd[:, 0:m], rm[0][:, 0:m], rm[1][:, 0:m], ALU.subtract).then_inc(rd_ready, 1)
                dve.tensor_tensor(both[:, 0:m, :], o1, o2, ALU.add).then_inc(both_ready, 1)
                if beside is not None:
                    low_x(beside + 1)
                dve.wait_ge(counted, gr + 1)
                pos = bank_a[:, 0:m * E].rearrange("p (t e) -> p t e", e=E)
                totp = bank_a[:, P:P + m * E].rearrange("p (t e) -> p e t", e=E)
                totg = tot[:].rearrange("p e t -> p (e t)")[:, 0:E * m]
                incg = inc[:].rearrange("p e t -> p (e t)")[:, 0:E * m]
                tot3, inc3 = (x.rearrange("p (e t) -> p e t", t=m) for x in (totg, incg))
                link(dve.tensor_copy(tot3, totp))
                link(dve.tensor_tensor_scan(incg, restart[m][:], totg, 0.0, ALU.mult, ALU.add))
                fill3 = fill[:].rearrange("p e t -> p (e t)")[:, 0:E * m].rearrange("p (e t) -> p e t", t=m)
                link(dve.tensor_tensor(fill3, inc3[:, :, m - 1:m].to_broadcast([P, E, m]),
                                       k128[:, 0:m].rearrange("p (a t) -> p a t", a=1).to_broadcast([P, E, m]),
                                       ALU.is_gt))
                link(dve.tensor_reduce(nti[:], fill3, AX.X, ALU.add))
                link(dve.tensor_tensor_scan(ends[:], ones_e, nti[:], 0.0, ALU.mult, ALU.add))
                link(dve.tensor_tensor(base[:], ends[:], nti[:], ALU.subtract))
                link(dve.tensor_scalar(base[:], base[:], float(P), float(N0[gr] * P), ALU.mult, ALU.add))
                link(dve.tensor_tensor(inc3, inc3, tot3, ALU.subtract))
                link(dve.tensor_tensor(inc3, inc3, base[:].rearrange("p (e a) -> p e a", a=1)
                                       .to_broadcast([P, E, m]), ALU.add))
                link(dve.tensor_tensor(spos[:, 0:m, :], pos, inc3.rearrange("p e t -> p t e"), ALU.add))
                link(dve.tensor_tensor(o1, o1, spos[:, 0:m, :], ALU.mult), wait=False)
                link(dve.tensor_tensor(o2, o2, spos[:, 0:m, :], ALU.mult))
                link(dve.tensor_reduce(slotf[:, 0, 0:m], o1, AX.X, ALU.add), wait=False)
                link(dve.tensor_reduce(slotf[:, 1, 0:m], o2, AX.X, ALU.add))
                J = SLOTS[gr]
                dve.tensor_copy(slots[:, :, t0:t0 + m], slotf[:, :, 0:m]).then_inc(slots_ready, 1)
                if beside is not None:
                    low_x(beside + 2)
                link(dve.tensor_tensor(ecmp[0:1, 0:J, :],
                                       ends[0:1, :].rearrange("p (a e) -> p a e", a=1).to_broadcast([1, J, E]),
                                       jidx[0:1, 0:J].rearrange("p (j a) -> p j a", a=1).to_broadcast([1, J, E]),
                                       ALU.is_le))
                link(dve.tensor_reduce(esum[0:1, 0:J], ecmp[0:1, 0:J, :], AX.X, ALU.add))
                for n0 in (N0[gr], N0[gr] + 1):
                    j0, b, k = n0 - N0[gr], n0 // 2, n0 % 2
                    cnt = (J - j0 + 1) // 2
                    for row, col in ((b, 2 + k), (b + 1, k)):
                        last = dve.tensor_scalar(eid[0:1, row:row + cnt, col], esum[0:1, j0:J:2], float(E - 1),
                                                 float(FF), ALU.min, ALU.mult)
                last.then_inc(experts_ready, 1)
                dve.wait_ge(rth_ready, gr + 1)
                dve.tensor_scalar(wts[:, 0, t0:t0 + m], rth[:, 0:m], 0.5, 0.5, ALU.mult, ALU.add)
                link(dve.tensor_scalar(wts[:, 1, t0:t0 + m], rth[:, 0:m], -0.5, 0.5, ALU.mult, ALU.add))

            ones_e = restart[min(restart)][:, 1:2].to_broadcast([P, E])

            def low_x(b):
                dve.wait_ge(xh_ready, b + 1)
                dve.tensor_tensor(xl[:], bank_x[:, 0:2 * P], xh[:].bitcast(f32), ALU.subtract).then_inc(xl_ready, 1)

            def close(j):
                apart = isinstance(j, int)
                has_o = not (apart and j < 2)
                has_u = not (apart and (j < 1 or j > NCH))
                has_z = not (apart and j >= NCH)
                if has_o:
                    dve.wait_ge(drs_ready, j)
                    at_least(dve, o_out, 16 * (j - 2))
                    for k in range(2):
                        last = dve.tensor_scalar(o_sb[:, k, :], u[:, k, :], mv_d[:, 2 + k, 0:1],
                                                 rs_d[:, 2 + k:3 + k], ALU.subtract, ALU.mult)
                    last.then_inc(o_ready, 1)
                if has_z:
                    if apart and j >= TAIL:
                        dve.wait_ge(gathering[j % 2], 64 * (j // 2 + 1))
                    else:
                        dve.wait_ge(gathered, j + 1)
                    at_least(dve, zn_ready, j)
                    src = [yg[:, bass.ds(j, 1), i, :].rearrange("p a e -> p (a e)") for i in range(4)]
                    w = [[wts[:, top, bass.ds(2 * j + k, 1)] for top in range(2)] for k in range(2)]
                    for k in range(2):
                        xk = x2[:, bass.ds(2 * j + k, 1), :].rearrange("p a e -> p (a e)")
                        last = dve.scalar_tensor_tensor(z[:, k, :], src[2 * k], w[k][0], xk, ALU.mult, ALU.add)
                    last.then_inc(za_ready, 1)
                if has_u:
                    dve.wait_ge(drs_ready, j)
                    dve.wait_ge(zn_ready, j)
                    dve.wait_ge(xb_ready, j)
                    if has_o:
                        dve.wait_ge(o_ready, j - 1)
                    for k in range(2):
                        last = dve.scalar_tensor_tensor(u[:, k, :], zn[:, k, :], rs_d[:, k:k + 1], xb[:, k, :],
                                                        ALU.mult, ALU.add)
                    last.then_inc(u_ready, 1)
                if has_z:
                    dve.wait_ge(za_ready, j + 1)
                    for k in range(2):
                        last = dve.scalar_tensor_tensor(z[:, k, :], src[2 * k + 1], w[k][1], z[:, k, :],
                                                        ALU.mult, ALU.add)
                    last.then_inc(z_done, 1)
                if has_u:
                    dve.wait_ge(u_ready, j)
                    for k in range(2):
                        last = dve.bn_stats(st_d[:, 2 + k, :], u[:, k, :])
                if has_z:
                    dve.wait_ge(z_done, j + 1)
                    for k in range(2):
                        last = dve.bn_stats(st_d[:, k, :], z[:, k, :])
                if not (has_u or has_z):
                    return
                last.then_inc(dst_ready, 1)
                if has_z:
                    dve.tensor_tensor(xb[:], x2[:, bass.ds(2 * j, 2), :],
                                      lnb.rearrange("p (a e) -> p a e", a=1).to_broadcast([P, 2, D]), ALU.add)\
                        .then_inc(xb_ready, 1)
                dve.wait_ge(dst_ready, j + 1)
                dve.memset(pace[:], 0.0)
                for k in range(0 if has_z else 2, 4 if has_u else 2):
                    last = dve.bn_aggr(mv_d[:, k, :], st_d[:, k, :])
                last.then_inc(dmv_ready, 1)
                dve.wait_ge(dmv_ready, j + 1)
                if has_u:
                    last = dve.tensor_scalar(ve_d[:, 2:4], mv_d[:, 2:4, 1], LN_EPS, None, ALU.add)
                if has_z:
                    last = dve.tensor_scalar(ve_d[:, 0:2], mv_d[:, 0:2, 1], FFN_EPS, None, ALU.add)
                last.then_inc(dvar_ready, 1)
                if has_z:
                    for k in range(2):
                        last = dve.scalar_tensor_tensor(zn[:, k, :], z[:, k, :], mv_d[:, k, 0:1], lnw,
                                                        ALU.subtract, ALU.mult)
                    last.then_inc(zn_ready, 1)

            def pair(b, before=None, behind=None):
                if before:
                    before()
                if not (isinstance(b, int) and b == PAIRS - 1):
                    low_x(b + 1)
                if behind:
                    behind()

            for seg in SCHEDULE:
                kind = seg[0]
                if kind in ("A", "AC"):
                    a0 = seg[-1] if kind == "AC" else seg[1]
                    n = seg[2]
                    for k in range(4):
                        if k * SEQ // CH in range(a0 + (a0 > 0), a0 + n + 1):
                            dve.wait_ge(x_in[k], 16)
                    if kind == "AC" and seg[1] == 0:
                        low_x(0)

                    def body(i, kind=kind, a0=a0, b0=seg[1]):
                        a = a0 + i
                        mix_2(a)
                        ahead = not (isinstance(a, int) and a == NCH - 1)
                        if ahead:
                            mix_1(a + 1)
                        if not (isinstance(i, int) and i == 0):
                            mix_4(a - 1)
                        if ahead:
                            mix_v(a + 1)
                        if kind == "AC":
                            pair(b0 + i)
                        mix_3(a)
                    if a0 == 0:
                        mix_1(0)
                        mix_v(0)
                    segment(dve, n, body, a0 + n == NCH)
                    mix_4(a0 + n - 1)
                elif kind == "R":
                    route_group(seg[1])
                elif kind == "RC":
                    route_group(seg[1], beside=seg[2])
                elif kind == "C":
                    segment(dve, seg[2], lambda i, b0=seg[1]: pair(b0 + i), seg[1] + seg[2] == PAIRS)
                elif kind == "DC":
                    _, b0, n, d0 = seg
                    segment(dve, n, lambda i, b0=b0, d0=d0: pair(b0 + i, behind=lambda: close(d0 + i)),
                            b0 + n == PAIRS, first=3 if d0 == 0 else 1)
                else:
                    for j in range(TAIL, NCH + 2):
                        close(j)


_INS = ["xT", "prm", "rows", "rwT", "w1T", "w2T", "b1", "b2"]


def kernel(**inputs):
    import numpy as np
    import concourse.bacc as bacc
    from concourse.bass_utils import run_bass_kernel_spmd

    x = {k: np.asarray(v) for k, v in inputs.items()}
    x = {k.replace("L0_attn_", "").replace("L0_ffn_", ""): v for k, v in x.items()}
    laid = {
        "xT": x["x"].reshape(T, D).T,
        "prm": np.concatenate([x[k].reshape(D, -1) for k in ("delta", "alpha", "beta", "gamma", "omega")], axis=1),
        "rows": np.concatenate([x[k].reshape(1, -1) for k in ("router_b", "ln_w", "ln_b")], axis=1),
        "rwT": x["router_w"].T,
        "w1T": x["w1"].transpose(2, 0, 1).reshape(D, E * FF),
        "w2T": x["w2"].reshape(E, D, FC, P).transpose(3, 0, 2, 1).reshape(P, E * FF),
        "b1": x["b1"].reshape(P, E * FF // P),
        "b2": x["b2"].reshape(P, E * D // P),
    }
    nc = bacc.Bacc("TRN2", target_bir_lowering=False, num_devices=1)
    arrays, args = {}, []
    for name in _INS:
        a = np.ascontiguousarray(laid[name])
        arrays[f"in_{name}"] = a
        args.append(nc.dram_tensor(f"in_{name}", a.shape, mybir.dt.from_np(a.dtype), kind="ExternalInput").ap())
    args.append(nc.dram_tensor("out_0", (T, D), f32, kind="ExternalOutput").ap())
    ema_moe_kernel(nc, *args)
    r = run_bass_kernel_spmd(nc, [arrays], core_ids=[0])
    return r.results[0]["out_0"].reshape(BATCH, SEQ, D)
```

```python
import math
from contextlib import ExitStack

import concourse.bass as bass
from concourse import mybir

f32 = mybir.dt.float32
bf16 = mybir.dt.bfloat16
i32 = mybir.dt.int32
ALU = mybir.AluOpType
ACT = mybir.ActivationFunctionType
AX = mybir.AxisListType

P = 128
BATCH, SEQ, D = 4, 1024, 128
T = BATCH * SEQ
E, FF, TOP = 8, 512, 2
FC = FF // P
WS = FF + FC
CH = 2 * P
NCH = T // CH
NT = T // P
CB = SEQ // CH
SCALE = math.sqrt(0.5)
LN_EPS, FFN_EPS = 1e-5, 1e-12
BIG = 3.0e38

GROUPS = [6, 8, 12, 6]
G = len(GROUPS)
T0 = [sum(GROUPS[:g]) for g in range(G + 1)]
SLOTS = [TOP * m + E - 1 for m in GROUPS]
N0 = [sum(SLOTS[:g]) for g in range(G + 1)]
NS = N0[G]
PAIRS = NS // 2
assert T0[G] == NT and NS % 2 == 0 and all(m % 2 == 0 for m in GROUPS)

SCHEDULE = [
    ("A", 0, 3), ("R", 0), ("A", 3, 3),
    ("AC", 0, 1, 6), ("RC", 1, 1, 2), ("AC", 3, 6, 7), ("RC", 2, 9, 3), ("AC", 12, 3, 13), ("RC", 3, 15, 3),
    ("C", 18, 9), ("DC", 27, 7, 0), ("C", 34, 5), ("DC", 39, 6, 7), ("C", 45, 1),
    ("D", 13),
]
POOL = [("a", 0), ("a", 1), ("a", 2)]
POOL += [("S", 0, 0, 4), ("a", 3), ("S", 0, 4, 4), ("a", 4), ("S", 0, 8, 4), ("a", 5), ("a", 6)]
POOL += [("S", 1, 0, 7), ("a", 7), ("S", 1, 7, 6), ("a", 8), ("S", 1, 13, 3)] + [("a", a) for a in range(9, 13)]
POOL += [("S", 2, 0, 6), ("a", 13), ("S", 2, 6, 4), ("a", 14), ("S", 2, 10, 5), ("a", 15), ("S", 2, 15, 9)]
POOL += [("g", 0), ("g", 1), ("S", 3, 0, 12)] + [("g", d) for d in range(2, 7)] + [("n", d) for d in range(7)]
POOL += [("p", d) for d in range(7)]
POOL += [("g", 7), ("g", 8), ("n", 7)]
for _d in range(7, 11):
    POOL += [("g", _d + 2), ("p", _d), ("n", _d + 1)]
POOL += [("p", 11), ("n", 12), ("p", 12), ("g", 13), ("g", 14), ("p", 13), ("g", 15)]
POOL += [("p", d) for d in range(14, 17)]
TAIL = SCHEDULE[-1][1]

PREP_DVE = 12
CONST = 10


def at_least(eng, sem, value):
    if not (isinstance(value, int) and value <= 0):
        eng.wait_ge(sem, value)


def repeat(eng, lo, hi, body):
    if hi - lo <= 1:
        for i in range(lo, hi):
            body(i)
    else:
        with eng.Fori(lo, hi) as i:
            body(i)


def segment(eng, n, body, last_apart=False, first=1):
    for i in range(min(first, n)):
        body(i)
    hi = n - 1 if last_apart and n > 1 else n
    repeat(eng, first, hi, body)
    if hi < n:
        body(n - 1)


def ema_moe_kernel(nc, xT, prm, rows, rwT, w1b, w2T, b2, out):
    xs_dram = nc.dram_tensor("slots_in", [NS * P, D], f32).ap()
    y_dram = nc.dram_tensor("slots_out", [NS * P, D], f32).ap()
    bias_dram = nc.dram_tensor("bias_parts", [3, E * D], bf16).ap()

    ctx = ExitStack()
    with ctx:
        def sb(name, shape, dt=f32):
            return ctx.enter_context(nc.sbuf_tensor(name, shape, dt))

        def sem(name):
            return ctx.enter_context(nc.semaphore(name))

        x_sb = sb("x_sb", [P, T])
        x2 = sb("x2", [P, NT, D])
        w1 = sb("w1", [P, E * WS])
        w2_all = sb("w2", [P, E, WS])
        w2 = w2_all[:].rearrange("p e f -> p (e f)")
        yg = sb("yg", [P, NCH, 2 * TOP, D])
        b2_all = sb("b2_rows", [P, E, WS], bf16)
        b2_rows = b2_all[:].rearrange("p e f -> p (e f)")
        bcol = sb("bcol", [P, E * D // P])
        bpart = sb("bpart", [P, 3, E * D // P], bf16)
        prm_sb = sb("prm_sb", [P, 9])
        row_sb = sb("row_sb", [P, E + 2 * D])
        rb, lnw, lnb = row_sb[:, 0:E], row_sb[:, E:E + D], row_sb[:, E + D:E + 2 * D]
        rw_sb, rwc = sb("rw_sb", [P, E]), sb("rwc", [P, E])
        zeros = sb("zeros", [P, 8 * D])
        ident, centre = sb("ident", [P, P]), sb("centre", [P, P])
        ones, before = sb("ones", [P, P], bf16), sb("before", [P, P], bf16)
        power = sb("power", [P, 4])
        pa, q, cf, om = sb("pa", [P, 4]), sb("q", [P, 2]), sb("cf", [P, 2]), sb("om", [P, 1])
        keep = sb("keep", [P, NCH + 1])
        carry = sb("carry", [P, 2])
        h = sb("h", [P, 2, CH])
        t1, t2, v, th, p, s = (sb(n, [P, CH]) for n in ("t1", "t2", "v", "th", "p", "s"))
        st_a, mv_a, ve_a, rs_a = sb("st_a", [P, 2, 6]), sb("mv_a", [P, 2, 2]), sb("ve_a", [P, 2]), sb("rs_a", [P, 2])
        M = max(GROUPS)
        logit = sb("logit", [P, NT, E])
        oh = [sb("oh1", [P, M, E]), sb("oh2", [P, M, E])]
        ra, rk = sb("ra", [P, M, E]), sb("rk", [P, M, E])
        rm = [sb("rm1", [P, M]), sb("rm2", [P, M])]
        rkm, rd, rth = sb("rkm", [P, M]), sb("rd", [P, M]), sb("rth", [P, M])
        both = sb("both", [P, M, E], bf16)
        tot, inc = sb("tot", [P, E, M]), sb("inc", [P, E, M])
        nti, ends, base = sb("nti", [P, E]), sb("ends", [P, E]), sb("base", [P, E])
        fill = sb("fill", [P, E, M])
        spos = sb("spos", [P, M, E])
        slotf = sb("slotf", [P, TOP, M])
        slots = sb("slots", [P, TOP, NT], i32)
        wts = sb("wts", [P, TOP, NT])
        rev = sb("rev", [P, E])
        k128 = sb("k128", [P, M])
        restart = {m: sb(f"restart{m}", [P, E * m]) for m in sorted(set(GROUPS))}
        JM = max(SLOTS)
        jidx, ecmp, esum = sb("jidx", [1, JM]), sb("ecmp", [1, JM, E]), sb("esum", [1, JM])
        eid = sb("eid", [1, PAIRS + 1, 4], i32)
        xs = sb("xs", [P, 2, D])
        xT_sb = sb("xT_sb", [P, 2 * P])
        w1_now = [sb(f"w1_now{k}", [P, WS]) for k in range(2)]
        gt = [sb(f"gt{k}", [P, FF]) for k in range(2)]
        y_sb = sb("y_sb", [P, 2, D])
        z, zn, u = sb("z", [P, 2, D]), sb("zn", [P, 2, D]), sb("u", [P, 2, D])
        xb = sb("xb", [P, 2, D])
        o_sb = sb("o_sb", [P, 2, D])
        st_d, mv_d, ve_d, rs_d = sb("st_d", [P, 4, 6]), sb("mv_d", [P, 4, 2]), sb("ve_d", [P, 4]), sb("rs_d", [P, 4])

        def pb(name):
            return ctx.enter_context(nc.psum_tensor(name, [P, 512], f32))

        bank_a, bank_x = pb("bank_a"), pb("bank_x")
        bank_z = [pb(f"bank_z{k}") for k in range(2)]
        bank_y = [pb(f"bank_y{k}") for k in range(2)]
        pace = sb("pace", [P, 1])
        stok = bank_a[:, 0:CH]
        raw = bank_a[:, CH:CH + 2 * E]

        prm_in, row_in, rw_in, b_in = sem("prm_in"), sem("row_in"), sem("rw_in"), sem("b_in")
        x_in = [sem(f"x_in{k}") for k in range(4)]
        w_in = [sem(f"w_in{k}") for k in range(4)]
        bias_out, bias_back = sem("bias_out"), sem("bias_back")
        cleared = [sem(f"cleared{k}") for k in range(G)]
        const = sem("const")
        pa_tanh = sem("pa_tanh")
        prep = sem("prep")
        rwc_ps = sem("rwc_ps")
        h1_ready, h2_ready, carry_ready = sem("h1_ready"), sem("h2_ready"), sem("carry_ready")
        t1_ready, t2_ready, v_ready, th_ready = sem("t1_ready"), sem("t2_ready"), sem("v_ready"), sem("th_ready")
        p_ready, s_ready, stok_ready = sem("p_ready"), sem("s_ready"), sem("stok_ready")
        st_ready, mv_ready, ve_ready, rs_ready = sem("st_ready"), sem("mv_ready"), sem("ve_ready"), sem("rs_ready")
        x2_ready = sem("x2_ready")
        route = sem("route")
        both_ready, counted, rd_ready, rth_ready = sem("both_ready"), sem("counted"), sem("rd_ready"), sem("rth_ready")
        slots_ready, experts_ready = sem("slots_ready"), sem("experts_ready")
        scattered = [sem(f"scattered{k}") for k in range(G)]
        xs_in, xsT_ready, xT_moved, w1_ready = sem("xs_in"), sem("xsT_ready"), sem("xT_moved"), sem("w1_ready")
        z_ready, gt_ready, y_ready, y_moved = sem("z_ready"), sem("gt_ready"), sem("y_ready"), sem("y_moved")
        y_out = [sem(f"y_out{k}") for k in range(2)]
        gathering = [sem(f"gathering{k}") for k in range(2)]
        gathered = sem("gathered")
        za_ready, z_done, dst_ready = sem("za_ready"), sem("z_done"), sem("dst_ready")
        dmv_ready, dvar_ready, drs_ready = sem("dmv_ready"), sem("dvar_ready"), sem("drs_ready")
        zn_ready, xb_ready, u_ready = sem("zn_ready"), sem("xb_ready"), sem("u_ready")
        o_ready, o_out = sem("o_ready"), sem("o_out")

        block = ctx.enter_context(nc.Block())

        @block.sync
        def _(sp):
            sp.dma_start(prm_sb[:], prm).then_inc(prm_in, 16)
            XP = T // 4
            sp.dma_start(x_sb[:, 0:XP], xT[:, 0:XP]).then_inc(x_in[0], 16)
            sp.dma_start(rw_sb[:], rwT).then_inc(rw_in, 16)
            sp.dma_start(row_sb[:], rows.to_broadcast([P, E + 2 * D])).then_inc(row_in, 16)
            sp.dma_start(bcol[:], b2).then_inc(b_in, 16)

            def clear(gr):
                for n in range(N0[gr], N0[gr + 1], 8):
                    k = min(8, N0[gr + 1] - n)
                    sp.dma_start(xs_dram[n * P:(n + k) * P, :].rearrange("(p r) d -> p (r d)", p=P),
                                 zeros[:, 0:k * D]).then_inc(cleared[gr], 16)

            sp.wait_ge(const, 1)
            clear(0)
            half = E * WS // 2
            for k in range(2):
                cols = slice(k * half, (k + 1) * half)
                sp.dma_start(w1[:, cols], w1b[:, cols]).then_inc(w_in[k], 16)
            sp.dma_start(x_sb[:, XP:2 * XP], xT[:, XP:2 * XP]).then_inc(x_in[1], 16)
            sp.wait_ge(prep, PREP_DVE)
            for r in range(3):
                sp.dma_start(bias_dram[r].rearrange("(p c) -> p c", p=P), bpart[:, r, :]).then_inc(bias_out, 16)
            for k in range(2):
                es = slice(k * E // 2, (k + 1) * E // 2)
                sp.dma_start(w2_all[:, es, 0:FF], w2T[:, es, :]).then_inc(w_in[2 + k], 16)
            sp.wait_ge(bias_out, 3 * 16)
            sp.wait_ge(const, CONST)
            sp.dma_start(b2_all[0:3, :, 0:D], bias_dram.rearrange("r (e d) -> r e d", e=E)).then_inc(bias_back, 16)
            for k in range(2, 4):
                sp.dma_start(x_sb[:, k * XP:(k + 1) * XP], xT[:, k * XP:(k + 1) * XP]).then_inc(x_in[k], 16)
            for gr in range(1, G):
                clear(gr)

            def load(b):
                at_least(sp, xsT_ready, b)
                sp.dma_start(xs[:], xs_dram[bass.ds(b * 2 * P, 2 * P), :].rearrange("(k p) d -> p k d", p=P))\
                    .then_inc(xs_in, 16)

            def store_y(n, k):
                sp.wait_ge(y_moved, n + 1)
                sp.dma_start(y_dram[bass.ds(n * P, P), :], y_sb[:, k, :]).then_inc(y_out[k], 16)

            def store_o(d):
                sp.wait_ge(o_ready, d + 1)
                sp.dma_start(out[bass.ds(d * CH, CH), :].rearrange("(k p) d -> p k d", p=P), o_sb[:])\
                    .then_inc(o_out, 16)

            def group_wait(b):
                for k in range(G):
                    if N0[k] // 2 == b:
                        sp.wait_ge(scattered[k], 16 * TOP * GROUPS[k])

            first_of = [N0[k] // 2 for k in range(G)]

            def pairs(b0, n, d0=None):
                at = b0
                while at < b0 + n:
                    if at + 2 in first_of and at + 2 < PAIRS:
                        group_wait(at + 2)
                    end = at + 1
                    while end < b0 + n and end + 2 not in first_of and (end + 2 < PAIRS) == (at + 2 < PAIRS) \
                            and at >= 1 and (d0 != 0 or at >= b0 + 2):
                        end += 1

                    def body(b, at=at):
                        if at + 2 < PAIRS:
                            load(b + 2)
                        if at >= 1:
                            store_y(2 * b - 1, 1)
                        store_y(2 * b, 0)
                        if d0 is not None and not (d0 == 0 and at < b0 + 2):
                            store_o(b - b0 + d0 - 2)
                    repeat(sp, at, end, body)
                    at = end

            group_wait(0)
            load(0)
            load(1)
            for seg in SCHEDULE:
                if seg[0] in ("C", "AC"):
                    pairs(seg[1], seg[2])
                elif seg[0] == "RC":
                    pairs(seg[2], seg[3])
                elif seg[0] == "DC":
                    _, b0, n, d0 = seg
                    pairs(b0, n, d0)
                elif seg[0] == "D":
                    store_y(NS - 1, 1)
                    repeat(sp, seg[1] - 2, NCH, store_o)
            sp.wait_ge(o_out, 16 * NCH)

        @block.gpsimd
        def _(pool):
            pool.memset(zeros[:], 0.0).then_inc(const, 1)
            pool.memset(ident[:], 0.0).then_inc(const, 1)
            pool.memset(ones[:], 1.0).then_inc(const, 1)
            pool.wait_ge(const, 3)
            pool.affine_select(out=ident[:], in_=ident[:], compare_op=ALU.not_equal, fill=1.0, base=0,
                               pattern=[[-1, P]], channel_multiplier=1).then_inc(const, 1)
            pool.affine_select(out=before[:], in_=ones[:], compare_op=ALU.is_gt, fill=0.0, base=0,
                               pattern=[[1, P]], channel_multiplier=-1).then_inc(const, 1)
            pool.memset(power[:], -0.5).then_inc(const, 1)
            imprecise = dict(channel_multiplier=0, allow_small_or_imprecise_dtypes=True)
            pool.iota(rev[:], pattern=[[-1, E]], base=E, **imprecise).then_inc(const, 1)
            pool.iota(k128[:], pattern=[[P, M]], base=0, **imprecise).then_inc(const, 1)
            pool.iota(jidx[:], pattern=[[1, JM]], base=0, **imprecise).then_inc(const, 1)
            pool.memset(b2_all[:, :, 0:D], 0.0).then_inc(const, 1)

            def scatter(gr, k0, n):
                if k0 == 0:
                    pool.wait_ge(slots_ready, gr + 1)
                    pool.wait_ge(cleared[gr], 16 * -(-SLOTS[gr] // 8))
                for k in range(k0, k0 + n):
                    t, top = T0[gr] + k // TOP, k % TOP
                    pool.indirect_dma_start(
                        out=xs_dram, out_offset=bass.IndirectOffsetOnAxis(ap=slots[:, top, t:t + 1], axis=0),
                        in_=x2[:, t, :], in_offset=None, bounds_check=NS * P - 1, oob_is_err=False,
                    ).then_inc(scattered[gr], 16)

            def gather(d):
                written = next(N0[gr + 1] * P for gr in range(G) if 2 * d < T0[gr + 1])
                for gr in range(G):
                    if 2 * d == T0[gr]:
                        pool.wait_ge(y_out[0], 16 * ((N0[gr + 1] + 1) // 2))
                        pool.wait_ge(y_out[1], 16 * (N0[gr + 1] // 2))
                if d >= 2:
                    pool.wait_ge(gathering[d % 2], 64 * (d // 2))
                for k in range(2):
                    for top in range(TOP):
                        pool.indirect_dma_start(
                            out=yg[:, d, 2 * k + top, :], out_offset=None, in_=y_dram[0:written, :],
                            in_offset=bass.IndirectOffsetOnAxis(ap=slots[:, top, 2 * d + k:2 * d + k + 1], axis=0),
                            bounds_check=written - 1, oob_is_err=False,
                        ).then_inc(gathering[d % 2], 16)

            for item in POOL:
                kind, d = item[0], item[1]
                if kind == "a":
                    pool.wait_ge(ve_ready, d + 1)
                    pool.tensor_tensor(rs_a[:], ve_a[:], power[:, 0:2], ALU.pow).then_inc(rs_ready, 1)
                elif kind == "S":
                    scatter(*item[1:])
                elif kind == "g":
                    gather(d)
                elif kind == "n":
                    pool.wait_ge(gathering[d % 2], 64 * (d // 2 + 1))
                    pool.engine_nop().then_inc(gathered, 1)
                else:
                    pool.wait_ge(dvar_ready, d + 1)
                    pool.tensor_tensor(rs_d[:], ve_d[:], power[:], ALU.pow).then_inc(drs_ready, 1)

        @block.scalar
        def _(act):
            act.wait_ge(prm_in, 16)
            act.activation(pa[:], prm_sb[:, 0:4], ACT.Tanh, scale=0.5).then_inc(pa_tanh, 1)

            def scale_h1(a):
                act.wait_ge(h1_ready, a + 1)
                if isinstance(a, int) and a == 0:
                    act.wait_ge(prep, 6)
                else:
                    act.wait_ge(t2_ready, a)
                act.activation(t1[:], h[:, 0, :], ACT.Copy, scale=cf[:, 0:1]).then_inc(t1_ready, 1)

            def tanh_v(a):
                act.wait_ge(v_ready, a + 1)
                at_least(act, p_ready, a)
                act.activation(th[:], v[:], ACT.Tanh).then_inc(th_ready, 1)

            def move_x(n, k, b):
                act.wait_ge(xsT_ready, b + 1)
                at_least(act, gt_ready, n - 1)
                cols = slice(k * P, (k + 1) * P)
                act.activation(xT_sb[:, cols], bank_x[:, cols], ACT.Copy).then_inc(xT_moved, 1)

            def experts(b):
                _, values = nc.values_load_multi_w_load_instructions(
                    eid[0:1, bass.ds(b, 1), :], engines=[mybir.EngineType.Activation], min_val=0,
                    max_val=(E - 1) * WS,
                    skip_runtime_bounds_check_because="counts of experts, kept to E - 1 by a minimum on the chip")
                return values

            def fetch_w1(k, e):
                act.activation(w1_now[k][:], w1[:, bass.ds(e, WS)], ACT.Copy).then_inc(w1_ready, 1)

            def gelu(n, k):
                act.wait_ge(z_ready, n + 1)
                at_least(act, y_ready, n - 1)
                for c in range(FC):
                    cols = slice(c * P, (c + 1) * P)
                    last = act.activation(gt[k][:, cols], bank_z[k][:, cols], ACT.Gelu,
                                          bias=w1_now[k][:, FF + c:FF + c + 1])
                last.then_inc(gt_ready, 1)

            def move_y(n, k, b):
                act.wait_ge(y_ready, n + 1)
                at_least(act, y_out[k], 16 * b)
                act.activation(y_sb[:, k, :], bank_y[k][:, 0:D], ACT.Copy).then_inc(y_moved, 1)

            def pair(b, a=None):
                first, last = isinstance(b, int) and b == 0, isinstance(b, int) and b == PAIRS - 1
                if isinstance(a, int) and a == NCH:
                    a = None
                gelu(2 * b, 0)
                if not last:
                    _, _, next0, next1 = experts(b + 1)
                if a is not None:
                    scale_h1(a)
                if not last:
                    move_x(2 * b + 2, 0, b + 1)
                    fetch_w1(0, next0)
                if not first:
                    move_y(2 * b - 1, 1, b - 1)
                gelu(2 * b + 1, 1)
                if a is not None:
                    tanh_v(a)
                if not last:
                    move_x(2 * b + 3, 1, b + 1)
                    fetch_w1(1, next1)
                move_y(2 * b, 0, b)

            for seg in SCHEDULE:
                kind = seg[0]
                if kind in ("AC", "C", "DC", "RC"):
                    b0, end = (seg[2], seg[2] + seg[3]) if kind == "RC" else (seg[1], seg[1] + seg[2])
                    for gr in range(G):
                        if b0 < N0[gr] // 2 <= end:
                            act.wait_ge(experts_ready, gr + 1)
                if kind == "A":
                    if seg[1] == 0:
                        scale_h1(0)
                        tanh_v(0)
                    repeat(act, seg[1] + 1, seg[1] + seg[2] + 1, lambda a: (scale_h1(a), tanh_v(a)))
                elif kind in ("R", "RC"):
                    gr = seg[1]
                    if kind == "RC":
                        for b in range(seg[2], seg[2] + seg[3]):
                            pair(b)
                    act.wait_ge(rd_ready, gr + 1)
                    act.activation(rth[:, 0:GROUPS[gr]], rd[:, 0:GROUPS[gr]], ACT.Tanh, scale=0.5)\
                        .then_inc(rth_ready, 1)
                elif kind == "AC":
                    _, b0, n, a0 = seg
                    if b0 == 0:
                        act.wait_ge(experts_ready, 1)
                        for k in range(2):
                            act.wait_ge(w_in[k], 16)
                        _, _, own0, own1 = experts(0)
                        for k, own in enumerate((own0, own1)):
                            fetch_w1(k, own)
                            move_x(k, k, 0)
                    segment(act, n, lambda i, b0=b0, a0=a0: pair(b0 + i, a0 + i + 1), a0 + n == NCH,
                            first=2 if b0 == 0 else 1)
                elif kind == "C":
                    segment(act, seg[2], lambda i, b0=seg[1]: pair(b0 + i), seg[1] + seg[2] == PAIRS)
                elif kind == "DC":
                    _, b0, n, d0 = seg
                    segment(act, n, lambda i, b0=b0: pair(b0 + i), b0 + n == PAIRS)

            move_y(NS - 1, 1, PAIRS - 1)

        @block.tensor
        def _(pe):
            pe.wait_ge(prep, 7)
            pe.wait_ge(rw_in, 16)
            pe.matmul(bank_a[:, 0:E], centre[:], rw_sb[:], start=True, stop=True).then_inc(rwc_ps, 1)
            pe.wait_ge(prep, 8)

            def turn_s(a):
                pe.wait_ge(s_ready, a + 1)
                at_least(pe, x2_ready, a)
                for k in range(2):
                    pe.transpose(stok[:, k * P:(k + 1) * P], s[:, k * P:(k + 1) * P], ident[:])
                for k in range(2):
                    last = pe.matmul(raw[:, k * E:(k + 1) * E], s[:, k * P:(k + 1) * P], rwc[:], start=True, stop=True)
                last.then_inc(stok_ready, 1)

            def turn_x(b):
                pe.wait_ge(xs_in, 16 * (b + 1))
                at_least(pe, xT_moved, 2 * b)
                for k in range(2):
                    last = pe.transpose(bank_x[:, k * P:(k + 1) * P], xs[:, k, :], ident[:])
                last.then_inc(xsT_ready, 1)

            def experts(b):
                _, values = nc.values_load_multi_w_load_instructions(
                    eid[0:1, bass.ds(b, 1), :], engines=[mybir.EngineType.PE], min_val=0, max_val=(E - 1) * WS,
                    skip_runtime_bounds_check_because="counts of experts, kept to E - 1 by a minimum on the chip")
                return values

            def up(b, k):
                pe.wait_ge(xT_moved, 2 * b + k + 1)
                pe.wait_ge(w1_ready, 2 * b + k + 1)
                at_least(pe, gt_ready, 2 * b + k - 1)
                for c in range(FC):
                    cols = slice(c * P, (c + 1) * P)
                    last = pe.matmul(bank_z[k][:, cols], w1_now[k][:, cols], xT_sb[:, k * P:(k + 1) * P],
                                     start=True, stop=True)
                last.then_inc(z_ready, 1)

            def down(n, k, e):
                pe.wait_ge(gt_ready, n + 1)
                at_least(pe, y_moved, n - 1)
                yb = bank_y[k][:, 0:D]
                for c in range(FC):
                    pe.matmul(yb, gt[k][:, c * P:(c + 1) * P], w2[:, bass.ds(e + c * P, P)],
                              start=(c == 0), stop=False)
                pe.matmul(yb, ones[:], b2_rows[:, bass.ds(e, D)], start=False, stop=True)\
                    .then_inc(y_ready, 1)

            def pair(b, a=None):
                first, last = isinstance(b, int) and b == 0, isinstance(b, int) and b == PAIRS - 1
                up(b, 0)
                _, before1, own0, _ = experts(b)
                if not last:
                    turn_x(b + 1)
                if not first:
                    down(2 * b - 1, 1, before1)
                up(b, 1)
                down(2 * b, 0, own0)
                if a is not None:
                    turn_s(a)

            for seg in SCHEDULE:
                kind = seg[0]
                if kind in ("AC", "C", "DC", "RC"):
                    b0, end = (seg[2], seg[2] + seg[3]) if kind == "RC" else (seg[1], seg[1] + seg[2])
                    for gr in range(G):
                        if b0 <= N0[gr] // 2 < end:
                            pe.wait_ge(experts_ready, gr + 1)
                if kind == "A":
                    segment(pe, seg[2], lambda i, a0=seg[1]: turn_s(a0 + i))
                elif kind in ("R", "RC"):
                    gr = seg[1]
                    m = GROUPS[gr]
                    if kind == "RC":
                        for b in range(seg[2], seg[2] + seg[3] - 1):
                            pair(b)
                    pe.wait_ge(both_ready, gr + 1)
                    pe.wait_ge(x2_ready, T0[gr + 1] // 2)
                    mm = both[:].rearrange("p t e -> p (t e)")[:, 0:m * E]
                    pe.matmul(bank_a[:, 0:m * E], before[:], mm, start=True, stop=True)
                    pe.matmul(bank_a[:, P:P + m * E], ones[:], mm, start=True, stop=True).then_inc(counted, 1)
                    if kind == "RC":
                        pair(seg[2] + seg[3] - 1)
                    pe.wait_ge(slots_ready, gr + 1)
                elif kind == "AC":
                    _, b0, n, a0 = seg
                    if b0 == 0:
                        turn_x(0)
                        for k in range(2, 4):
                            pe.wait_ge(w_in[k], 16)
                        pe.wait_ge(bias_back, 16)
                    segment(pe, n, lambda i, b0=b0, a0=a0: pair(b0 + i, a0 + i), first=2 if b0 == 0 else 1)
                elif kind == "C":
                    segment(pe, seg[2], lambda i, b0=seg[1]: pair(b0 + i), seg[1] + seg[2] == PAIRS)
                elif kind == "DC":
                    _, b0, n, d0 = seg
                    segment(pe, n, lambda i, b0=b0: pair(b0 + i), b0 + n == PAIRS)

            _, before1, _, _ = experts(PAIRS)
            down(NS - 1, 1, before1)

        @block.vector
        def _(dve):
            steps = [0]

            def prepared(ins):
                ins.then_inc(prep, 1)
                steps[0] += 1

            dve.memset(carry[:], 0.0).then_inc(carry_ready, 1)
            dve.memset(keep[:], 1.0).then_inc(route, 1)
            dve.memset(ve_d[:], 1.0).then_inc(route, 1)
            dve.memset(eid[:], 0).then_inc(route, 1)
            for m in restart:
                dve.memset(restart[m][:], 1.0).then_inc(route, 1)
            ROUTE0 = 3 + len(restart)
            dve.wait_ge(route, ROUTE0)
            dve.memset(keep[:, 0:NCH + 1:CB], 0.0).then_inc(route, 1)
            for m in restart:
                dve.memset(restart[m][:, 0:E * m:m], 0.0).then_inc(route, 1)
            ROUTE0 += 1 + len(restart)
            rc = [ROUTE0]

            def link(ins, wait=True):
                rc[0] += 1
                ins.then_inc(route, 1)
                if wait:
                    dve.wait_ge(route, rc[0])

            dve.wait_ge(pa_tanh, 1)
            prepared(dve.tensor_scalar(pa[:], pa[:], 0.5, 0.5, ALU.mult, ALU.add))
            dve.wait_ge(prep, 1)
            prepared(dve.tensor_tensor(q[:], pa[:, 0:2], pa[:, 2:4], ALU.mult))
            prepared(dve.tensor_tensor(cf[:], pa[:, 0:2], prm_sb[:, 4:6], ALU.mult))
            dve.wait_ge(prep, 3)
            prepared(dve.tensor_scalar(q[:], q[:], -1.0, 1.0, ALU.mult, ALU.add))
            prepared(dve.tensor_scalar(om[:], prm_sb[:, 8:9], 0.5, None, ALU.mult))
            prepared(dve.scalar_tensor_tensor(cf[:], cf[:], 0.5 * SCALE, prm_sb[:, 6:8], ALU.mult, ALU.mult))
            dve.wait_ge(const, 9)
            prepared(dve.tensor_scalar(centre[:], ident[:], -1.0 / D, None, ALU.add))
            dve.wait_ge(rwc_ps, 1)
            prepared(dve.tensor_copy(rwc[:], bank_a[:, 0:E]))
            dve.wait_ge(b_in, 16)
            prepared(dve.tensor_copy(bpart[:, 0, :], bcol[:]))
            dve.wait_ge(prep, 9)
            prepared(dve.tensor_tensor(bcol[:], bcol[:], bpart[:, 0, :], ALU.subtract))
            dve.wait_ge(prep, 10)
            prepared(dve.tensor_copy(bpart[:, 1, :], bcol[:]))
            dve.wait_ge(prep, 11)
            prepared(dve.tensor_tensor(bpart[:, 2, :], bcol[:], bpart[:, 1, :], ALU.subtract))
            dve.wait_ge(prep, PREP_DVE)
            assert steps[0] == PREP_DVE

            def mix_1(a):
                xc = x_sb[:, bass.ds(a * CH, CH)]
                dve.wait_ge(carry_ready, a + 1)
                for n, ready in ((0, h1_ready), (1, h2_ready)):
                    dve.tensor_tensor_scan(h[:, n, :], q[:, n:n + 1].to_broadcast([P, CH]), xc,
                                           carry[:, n:n + 1], ALU.mult, ALU.add).then_inc(ready, 1)
                dve.wait_ge(h2_ready, a + 1)
                dve.tensor_tensor(carry[:], h[:, :, CH - 1], keep[:, bass.ds(a + 1, 1)].to_broadcast([P, 2]),
                                  ALU.mult).then_inc(carry_ready, 1)

            def mix_v(a):
                xc = x_sb[:, bass.ds(a * CH, CH)]
                dve.wait_ge(t1_ready, a + 1)
                dve.scalar_tensor_tensor(t2[:], h[:, 1, :], cf[:, 1:2], t1[:], ALU.mult, ALU.add)\
                    .then_inc(t2_ready, 1)
                dve.wait_ge(t2_ready, a + 1)
                dve.scalar_tensor_tensor(v[:], xc, om[:, 0:1], t2[:], ALU.mult, ALU.add).then_inc(v_ready, 1)

            def mix_2(a):
                xc = x_sb[:, bass.ds(a * CH, CH)]
                dve.wait_ge(th_ready, a + 1)
                dve.scalar_tensor_tensor(p[:], th[:], 1.0, v[:], ALU.add, ALU.mult).then_inc(p_ready, 1)
                dve.wait_ge(p_ready, a + 1)
                dve.tensor_tensor(s[:], p[:], xc, ALU.add).then_inc(s_ready, 1)

            def mix_3(a):
                dve.wait_ge(stok_ready, a + 1)
                for k in range(2):
                    last = dve.bn_stats(st_a[:, k, :], stok[:, k * P:(k + 1) * P])
                last.then_inc(st_ready, 1)
                dve.wait_ge(st_ready, a + 1)
                dve.memset(pace[:], 0.0)
                for k in range(2):
                    last = dve.bn_aggr(mv_a[:, k, :], st_a[:, k, :])
                last.then_inc(mv_ready, 1)
                dve.wait_ge(mv_ready, a + 1)
                dve.tensor_scalar(ve_a[:], mv_a[:, :, 1], LN_EPS, None, ALU.add).then_inc(ve_ready, 1)

            def mix_4(a):
                dve.wait_ge(rs_ready, a + 1)
                for k in range(2):
                    dve.tensor_scalar(logit[:, bass.ds(2 * a + k, 1), :].rearrange("p a e -> p (a e)"),
                                      raw[:, k * E:(k + 1) * E], rs_a[:, k:k + 1], None, ALU.mult)
                for k in range(2):
                    last = dve.tensor_scalar(x2[:, bass.ds(2 * a + k, 1), :].rearrange("p a e -> p (a e)"),
                                             stok[:, k * P:(k + 1) * P], mv_a[:, k, 0:1], rs_a[:, k:k + 1],
                                             ALU.subtract, ALU.mult)
                last.then_inc(x2_ready, 1)

            def route_group(gr):
                m, t0 = GROUPS[gr], T0[gr]
                full = [P, m, E]
                lg = logit[:, t0:t0 + m, :]
                o1, o2, wa, wk = (x[:, 0:m, :] for x in (oh[0], oh[1], ra, rk))
                revb = rev[:, :].rearrange("p (a e) -> p a e", a=1).to_broadcast(full)

                def over_e(x):
                    return x[:, 0:m].rearrange("p (t a) -> p t a", a=1).to_broadcast(full)

                def first_max(src, mx, o):
                    link(dve.tensor_reduce(mx[:, 0:m], src, AX.X, ALU.max))
                    link(dve.tensor_tensor(wk, src, over_e(mx), ALU.is_equal))
                    link(dve.tensor_tensor(wk, wk, revb, ALU.mult))
                    link(dve.tensor_reduce(rkm[:, 0:m], wk, AX.X, ALU.max))
                    link(dve.tensor_tensor(o, wk, over_e(rkm), ALU.is_equal))

                if gr == 0:
                    dve.wait_ge(row_in, 16)
                dve.wait_ge(x2_ready, (t0 + m) // 2)
                link(dve.tensor_tensor(lg, lg, rb.rearrange("p (a e) -> p a e", a=1).to_broadcast(full), ALU.add))
                first_max(lg, rm[0], o1)
                link(dve.tensor_scalar(wa, o1, -BIG, 0.5 * BIG, ALU.mult, ALU.add))
                link(dve.tensor_tensor(wa, wa, lg, ALU.min))
                first_max(wa, rm[1], o2)
                dve.tensor_tensor(rd[:, 0:m], rm[0][:, 0:m], rm[1][:, 0:m], ALU.subtract).then_inc(rd_ready, 1)
                dve.tensor_tensor(both[:, 0:m, :], o1, o2, ALU.add).then_inc(both_ready, 1)
                dve.wait_ge(counted, gr + 1)
                pos = bank_a[:, 0:m * E].rearrange("p (t e) -> p t e", e=E)
                totp = bank_a[:, P:P + m * E].rearrange("p (t e) -> p e t", e=E)
                totg = tot[:].rearrange("p e t -> p (e t)")[:, 0:E * m]
                incg = inc[:].rearrange("p e t -> p (e t)")[:, 0:E * m]
                tot3, inc3 = (x.rearrange("p (e t) -> p e t", t=m) for x in (totg, incg))
                link(dve.tensor_copy(tot3, totp))
                link(dve.tensor_tensor_scan(incg, restart[m][:], totg, 0.0, ALU.mult, ALU.add))
                fill3 = fill[:].rearrange("p e t -> p (e t)")[:, 0:E * m].rearrange("p (e t) -> p e t", t=m)
                link(dve.tensor_tensor(fill3, inc3[:, :, m - 1:m].to_broadcast([P, E, m]),
                                       k128[:, 0:m].rearrange("p (a t) -> p a t", a=1).to_broadcast([P, E, m]),
                                       ALU.is_gt))
                link(dve.tensor_reduce(nti[:], fill3, AX.X, ALU.add))
                link(dve.tensor_tensor_scan(ends[:], ones_e, nti[:], 0.0, ALU.mult, ALU.add))
                link(dve.tensor_tensor(base[:], ends[:], nti[:], ALU.subtract))
                link(dve.tensor_scalar(base[:], base[:], float(P), float(N0[gr] * P), ALU.mult, ALU.add))
                link(dve.tensor_tensor(inc3, inc3, tot3, ALU.subtract))
                link(dve.tensor_tensor(inc3, inc3, base[:].rearrange("p (e a) -> p e a", a=1)
                                       .to_broadcast([P, E, m]), ALU.add))
                link(dve.tensor_tensor(spos[:, 0:m, :], pos, inc3.rearrange("p e t -> p t e"), ALU.add))
                link(dve.tensor_tensor(o1, o1, spos[:, 0:m, :], ALU.mult), wait=False)
                link(dve.tensor_tensor(o2, o2, spos[:, 0:m, :], ALU.mult))
                link(dve.tensor_reduce(slotf[:, 0, 0:m], o1, AX.X, ALU.add), wait=False)
                link(dve.tensor_reduce(slotf[:, 1, 0:m], o2, AX.X, ALU.add))
                J = SLOTS[gr]
                dve.tensor_copy(slots[:, :, t0:t0 + m], slotf[:, :, 0:m]).then_inc(slots_ready, 1)
                link(dve.tensor_tensor(ecmp[0:1, 0:J, :],
                                       ends[0:1, :].rearrange("p (a e) -> p a e", a=1).to_broadcast([1, J, E]),
                                       jidx[0:1, 0:J].rearrange("p (j a) -> p j a", a=1).to_broadcast([1, J, E]),
                                       ALU.is_le))
                link(dve.tensor_reduce(esum[0:1, 0:J], ecmp[0:1, 0:J, :], AX.X, ALU.add))
                for n0 in (N0[gr], N0[gr] + 1):
                    j0, b, k = n0 - N0[gr], n0 // 2, n0 % 2
                    cnt = (J - j0 + 1) // 2
                    for row, col in ((b, 2 + k), (b + 1, k)):
                        last = dve.tensor_scalar(eid[0:1, row:row + cnt, col], esum[0:1, j0:J:2], float(E - 1),
                                                 float(WS), ALU.min, ALU.mult)
                last.then_inc(experts_ready, 1)
                dve.wait_ge(rth_ready, gr + 1)
                dve.tensor_scalar(wts[:, 0, t0:t0 + m], rth[:, 0:m], 0.5, 0.5, ALU.mult, ALU.add)
                link(dve.tensor_scalar(wts[:, 1, t0:t0 + m], rth[:, 0:m], -0.5, 0.5, ALU.mult, ALU.add))

            ones_e = restart[min(restart)][:, 1:2].to_broadcast([P, E])

            def close(j):
                apart = isinstance(j, int)
                has_o = not (apart and j < 2)
                has_u = not (apart and (j < 1 or j > NCH))
                has_z = not (apart and j >= NCH)
                if has_o:
                    dve.wait_ge(drs_ready, j)
                    at_least(dve, o_out, 16 * (j - 2))
                    for k in range(2):
                        last = dve.tensor_scalar(o_sb[:, k, :], u[:, k, :], mv_d[:, 2 + k, 0:1],
                                                 rs_d[:, 2 + k:3 + k], ALU.subtract, ALU.mult)
                    last.then_inc(o_ready, 1)
                if has_z:
                    if apart and j >= TAIL:
                        dve.wait_ge(gathering[j % 2], 64 * (j // 2 + 1))
                    else:
                        dve.wait_ge(gathered, j + 1)
                    at_least(dve, zn_ready, j)
                    src = [yg[:, bass.ds(j, 1), i, :].rearrange("p a e -> p (a e)") for i in range(4)]
                    w = [[wts[:, top, bass.ds(2 * j + k, 1)] for top in range(2)] for k in range(2)]
                    for k in range(2):
                        xk = x2[:, bass.ds(2 * j + k, 1), :].rearrange("p a e -> p (a e)")
                        last = dve.scalar_tensor_tensor(z[:, k, :], src[2 * k], w[k][0], xk, ALU.mult, ALU.add)
                    last.then_inc(za_ready, 1)
                if has_u:
                    dve.wait_ge(drs_ready, j)
                    dve.wait_ge(zn_ready, j)
                    dve.wait_ge(xb_ready, j)
                    if has_o:
                        dve.wait_ge(o_ready, j - 1)
                    for k in range(2):
                        last = dve.scalar_tensor_tensor(u[:, k, :], zn[:, k, :], rs_d[:, k:k + 1], xb[:, k, :],
                                                        ALU.mult, ALU.add)
                    last.then_inc(u_ready, 1)
                if has_z:
                    dve.wait_ge(za_ready, j + 1)
                    for k in range(2):
                        last = dve.scalar_tensor_tensor(z[:, k, :], src[2 * k + 1], w[k][1], z[:, k, :],
                                                        ALU.mult, ALU.add)
                    last.then_inc(z_done, 1)
                if has_u:
                    dve.wait_ge(u_ready, j)
                    for k in range(2):
                        last = dve.bn_stats(st_d[:, 2 + k, :], u[:, k, :])
                if has_z:
                    dve.wait_ge(z_done, j + 1)
                    for k in range(2):
                        last = dve.bn_stats(st_d[:, k, :], z[:, k, :])
                if not (has_u or has_z):
                    return
                last.then_inc(dst_ready, 1)
                if has_z:
                    dve.tensor_tensor(xb[:], x2[:, bass.ds(2 * j, 2), :],
                                      lnb.rearrange("p (a e) -> p a e", a=1).to_broadcast([P, 2, D]), ALU.add)\
                        .then_inc(xb_ready, 1)
                dve.wait_ge(dst_ready, j + 1)
                dve.memset(pace[:], 0.0)
                for k in range(0 if has_z else 2, 4 if has_u else 2):
                    last = dve.bn_aggr(mv_d[:, k, :], st_d[:, k, :])
                last.then_inc(dmv_ready, 1)
                dve.wait_ge(dmv_ready, j + 1)
                if has_u:
                    last = dve.tensor_scalar(ve_d[:, 2:4], mv_d[:, 2:4, 1], LN_EPS, None, ALU.add)
                if has_z:
                    last = dve.tensor_scalar(ve_d[:, 0:2], mv_d[:, 0:2, 1], FFN_EPS, None, ALU.add)
                last.then_inc(dvar_ready, 1)
                if has_z:
                    for k in range(2):
                        last = dve.scalar_tensor_tensor(zn[:, k, :], z[:, k, :], mv_d[:, k, 0:1], lnw,
                                                        ALU.subtract, ALU.mult)
                    last.then_inc(zn_ready, 1)

            for seg in SCHEDULE:
                kind = seg[0]
                if kind in ("A", "AC"):
                    a0 = seg[-1] if kind == "AC" else seg[1]
                    n = seg[2]
                    for k in range(4):
                        if k * SEQ // CH in range(a0 + (a0 > 0), a0 + n + 1):
                            dve.wait_ge(x_in[k], 16)

                    def body(i, a0=a0):
                        a = a0 + i
                        mix_2(a)
                        ahead = not (isinstance(a, int) and a == NCH - 1)
                        if ahead:
                            mix_1(a + 1)
                        if not (isinstance(i, int) and i == 0):
                            mix_4(a - 1)
                        if ahead:
                            mix_v(a + 1)
                        mix_3(a)
                    if a0 == 0:
                        mix_1(0)
                        mix_v(0)
                    segment(dve, n, body, a0 + n == NCH)
                    mix_4(a0 + n - 1)
                elif kind in ("R", "RC"):
                    route_group(seg[1])
                elif kind == "DC":
                    _, _, n, d0 = seg
                    segment(dve, n, lambda i, d0=d0: close(d0 + i), first=3 if d0 == 0 else 1)
                elif kind == "D":
                    for j in range(TAIL, NCH + 2):
                        close(j)


_INS = ["xT", "prm", "rows", "rwT", "w1b", "w2T", "b2"]


def kernel(**inputs):
    import numpy as np
    import concourse.bacc as bacc
    from concourse.bass_utils import run_bass_kernel_spmd

    x = {k: np.asarray(v) for k, v in inputs.items()}
    x = {k.replace("L0_attn_", "").replace("L0_ffn_", ""): v for k, v in x.items()}
    laid = {
        "xT": x["x"].reshape(T, D).T,
        "prm": np.concatenate([x[k].reshape(D, -1) for k in ("delta", "alpha", "beta", "gamma", "omega")], axis=1),
        "rows": np.concatenate([x[k].reshape(1, -1) for k in ("router_b", "ln_w", "ln_b")], axis=1),
        "rwT": x["router_w"].T,
        "w1b": np.concatenate([x["w1"].transpose(2, 0, 1), x["b1"].reshape(E, FC, P).transpose(2, 0, 1)],
                              axis=2).reshape(D, E * WS),
        "w2T": x["w2"].reshape(E, D, FC, P).transpose(3, 0, 2, 1).reshape(P, E, FF),
        "b2": x["b2"].reshape(P, E * D // P),
    }
    nc = bacc.Bacc("TRN2", target_bir_lowering=False, num_devices=1)
    arrays, args = {}, []
    for name in _INS:
        a = np.ascontiguousarray(laid[name])
        arrays[f"in_{name}"] = a
        args.append(nc.dram_tensor(f"in_{name}", a.shape, mybir.dt.from_np(a.dtype), kind="ExternalInput").ap())
    args.append(nc.dram_tensor("out_0", (T, D), f32, kind="ExternalOutput").ap())
    ema_moe_kernel(nc, *args)
    r = run_bass_kernel_spmd(nc, [arrays], core_ids=[0])
    return r.results[0]["out_0"].reshape(BATCH, SEQ, D)
```
